# Optimizing a Trainium2 kernel written in Bass

```python
import numpy as np
import jax
import jax.numpy as jnp

def _softmax(x, axis=-1):
    return jax.nn.softmax(x, axis=axis)

def _gelu(x):
    return jax.nn.gelu(x, approximate=True)

def _silu(x):
    return jax.nn.silu(x)

def _sigmoid(x):
    return jax.nn.sigmoid(x)

def _layernorm(x, axis=-1, eps=1e-05):
    m = jnp.mean(x, axis=axis, keepdims=True)
    v = jnp.var(x, axis=axis, keepdims=True)
    return (x - m) / jnp.sqrt(v + eps)

def _scatter_add(tgt, idx, src, axis=0):
    return tgt.at[idx].add(src)

def _segment_sum(src, seg, n):
    return jax.ops.segment_sum(src, seg, n)
kernel_name = 'mk_adj_resnorm_d1_adj_r2_dda808'

def setup_inputs(seed: int=0):
    np.random.seed(seed)
    _w = jnp.asarray

    def _rec_inputs():
        import jax
        import jax.numpy as jnp
        _gk = jax.random.key(seed)
        x = -0.001003 + 1 * jax.random.normal(jax.random.fold_in(_gk, 1), (64, 128, 384), jnp.float32)
        _a = jax.random.bernoulli(jax.random.fold_in(_gk, 2), 0.0625, (64, 128, 128))
        _a = jnp.logical_or(_a, jnp.swapaxes(_a, -1, -2))
        _a = jnp.logical_or(_a, jnp.eye(128, dtype=bool))
        adj = _a.astype(jnp.int32)
        return (x, adj)
    x, adj = _rec_inputs()

    def _L0_gnn_setup():
        import jax, jax.numpy as jnp
        import numpy as np
        B, L, H = (8, 128, 384)
        R = 128
        NUM_REL = 80
        NUM_BASE = NUM_REL // 2
        key = jax.random.key(seed)
        ks = jax.random.split(key, 12)
        s = 0.02
        E = jax.random.normal(ks[3], (NUM_REL, R), jnp.float32) * s
        E = E.at[0].set(0.0)
        return {'hidden_states': jax.random.normal(ks[0], (B, L, H), jnp.float32), 'heads': jax.random.randint(ks[1], (B, L, L), 0, 2), 'rels': jax.random.randint(ks[2], (B, L, L), 0, NUM_BASE), 'E': E, 'Wadj': jax.random.normal(ks[4], (H, H), jnp.float32) * s, 'badj': jnp.zeros((H,), jnp.float32), 'Wrev': jax.random.normal(ks[5], (H, H), jnp.float32) * s, 'brev': jnp.zeros((H,), jnp.float32), 'Wself': jax.random.normal(ks[6], (H, H), jnp.float32) * s, 'bself': jnp.zeros((H,), jnp.float32), 'Wr': jax.random.normal(ks[7], (H, R), jnp.float32) * s, 'br': jnp.zeros((H,), jnp.float32), 'Wrr': jax.random.normal(ks[8], (H, R), jnp.float32) * s, 'brr': jnp.zeros((H,), jnp.float32)}
    _L0_gnn_all = _L0_gnn_setup()
    _L0_gnn_in = {k: v for k, v in _L0_gnn_all.items() if k in ('E', 'Wadj', 'badj', 'Wrev', 'brev', 'Wself', 'bself', 'Wr', 'br', 'Wrr', 'brr')}
    del _L0_gnn_all
    return {'x': x, 'adj': adj, 'L0_gnn_E': _L0_gnn_in['E'], 'L0_gnn_Wadj': _L0_gnn_in['Wadj'], 'L0_gnn_badj': _L0_gnn_in['badj'], 'L0_gnn_Wrev': _L0_gnn_in['Wrev'], 'L0_gnn_brev': _L0_gnn_in['brev'], 'L0_gnn_Wself': _L0_gnn_in['Wself'], 'L0_gnn_bself': _L0_gnn_in['bself'], 'L0_gnn_Wr': _L0_gnn_in['Wr'], 'L0_gnn_br': _L0_gnn_in['br'], 'L0_gnn_Wrr': _L0_gnn_in['Wrr'], 'L0_gnn_brr': _L0_gnn_in['brr']}

def reference(x, adj, L0_gnn_E, L0_gnn_Wadj, L0_gnn_badj, L0_gnn_Wrev, L0_gnn_brev, L0_gnn_Wself, L0_gnn_bself, L0_gnn_Wr, L0_gnn_br, L0_gnn_Wrr, L0_gnn_brr):
    import jax
    import jax.numpy as jnp

    def _L0_gnn_ref(hidden_states, heads, rels, E, Wadj, badj, Wrev, brev, Wself, bself, Wr, br, Wrr, brr):
        import jax, jax.numpy as jnp
        import numpy as np
        B, L, H = (8, 128, 384)
        R = 128
        NUM_REL = 80
        NUM_BASE = NUM_REL // 2
        hs = hidden_states
        adj = heads.astype(hs.dtype)
        radj = jnp.swapaxes(adj, 1, 2)
        deg = adj.sum(-1)
        rdeg = radj.sum(-1)
        deg_c = jnp.where(deg > 0, deg, 1.0)
        rdeg_c = jnp.where(rdeg > 0, rdeg, 1.0)
        ctx = jnp.matmul(adj, hs @ Wadj.T + badj) / deg_c[..., None]
        ctx = ctx + jnp.matmul(radj, hs @ Wrev.T + brev) / rdeg_c[..., None]
        ctx = ctx + hs @ Wself.T + bself
        agg = jnp.einsum('bij,bijr->bir', adj, E[rels])
        rel = agg @ Wr.T + br * deg[..., None]
        rr = jnp.swapaxes(rels, 1, 2) + NUM_BASE
        rr = jnp.where(rr > NUM_BASE, rr, 0)
        ragg = jnp.einsum('bij,bijr->bir', radj, E[rr])
        rel = rel + ragg @ Wrr.T + brr * rdeg[..., None]
        return ctx + rel
    x = _layernorm(x + _L0_gnn_ref(x, adj, adj, L0_gnn_E, L0_gnn_Wadj, L0_gnn_badj, L0_gnn_Wrev, L0_gnn_brev, L0_gnn_Wself, L0_gnn_bself, L0_gnn_Wr, L0_gnn_br, L0_gnn_Wrr, L0_gnn_brr), axis=-1)
    return x

_drawn_inputs = setup_inputs


def setup_inputs(seed=0):
    import zlib

    import numpy as np

    out = dict(_drawn_inputs(seed))
    spreads = {'L0_gnn_badj': (0.0, 0.1),
     'L0_gnn_brev': (0.0, 0.1),
     'L0_gnn_bself': (0.0, 0.1),
     'L0_gnn_br': (0.0, 0.1),
     'L0_gnn_brr': (0.0, 0.1)}
    factors = {}
    for name, (base, spread) in spreads.items():
        noise = np.random.default_rng([zlib.crc32(name.encode()), seed]).standard_normal(out[name].shape)
        drawn = base * np.exp(spread * noise) if base else spread * noise
        out[name] = jnp.asarray(drawn.astype(out[name].dtype))
    for name, factor in factors.items():
        out[name] = (out[name] * factor).astype(out[name].dtype)
    return out
```

```python
from contextlib import ExitStack

import concourse.bass as bass
from concourse import mybir

fp32 = mybir.dt.float32
fp32r = mybir.dt.float32r
i32 = mybir.dt.int32
ALU = mybir.AluOpType
ACT = mybir.ActivationFunctionType
AX = mybir.AxisListType

B, N, H = 64, 128, 384
R = 128
NUM_REL, NUM_BASE = 80, 40
P = 128
HC = H // P
G = 4
NG = B // G
UNROLL = 2 * G
ITERS = B // UNROLL
EPS = 1e-5
NORM_LAG = 7
KB = 64
LOW = 32

C_ID, C_IOTA = 0, P
C_SEL_R = C_IOTA + NUM_REL
C_SEL_RR = C_SEL_R + KB
C_SEL_B = C_SEL_RR + KB
C_LIM = C_SEL_B + KB
C_ONE = C_LIM + 2
C_END = C_ONE + P


def constants():
    import numpy as np

    t = np.zeros((P, C_END), np.float32)
    t[:, C_ID:C_ID + P] = np.eye(P)
    t[:, C_IOTA:C_IOTA + NUM_REL] = np.arange(NUM_REL)
    t[:, C_ONE:C_ONE + P] = 1.0
    for m in (0, LOW):
        t[[1, NUM_REL], C_SEL_R + m] = 1.0
        t[[NUM_BASE + 1, NUM_REL], C_SEL_RR + m] = 1.0
        t[2, C_SEL_B + m + 1] = 1.0
        t[[0, 1], C_SEL_B + m + 2] = 1.0
        t[m, C_LIM:C_LIM + 2] = 0.0, N
        t[m + 1, C_LIM:C_LIM + 2] = 1.0, 1.0
        t[m + 2, C_LIM:C_LIM + 2] = 0.0, 1.0
    return t


def graph_layer(nc, x, adj, ET, WadjT, badj, WrevT, brev, WselfT, bself, WrT, br, WrrT, brr, table, out):
    x_groups = x.rearrange("(g e) i h -> g i e h", e=G)
    adj_groups = adj.rearrange("(g e) i j -> g i e j", e=G)
    out_groups = out.rearrange("(g e) i h -> g i e h", e=G)

    with ExitStack() as ctx:
        def sb(name, shape, dt=fp32):
            return ctx.enter_context(nc.sbuf_tensor(name, shape, dt))

        def sem(name):
            return ctx.enter_context(nc.semaphore(name))

        tab = sb("tab", [P, C_END])
        ident = tab[:, C_ID:C_ID + P]
        ones_r = sb("ones_r", [P, P], fp32r)
        w_adj = sb("w_adj", [P, HC, H])
        w_rev = sb("w_rev", [P, HC, H])
        w_self = sb("w_self", [P, HC, H])
        w_nb = sb("w_nb", [P, HC, H])
        nb_hi = sb("nb_hi", [P, HC, H], fp32r)
        nb_lo = sb("nb_lo", [P, HC, H], fp32r)
        self_hi = sb("self_hi", [P, HC, H], fp32r)
        self_lo = sb("self_lo", [P, HC, H], fp32r)
        e_t = sb("e_t", [R, NUM_REL])
        wr_t = sb("wr_t", [R, H])
        wrr_t = sb("wrr_t", [R, H])
        ew_r = sb("ew_r", [NUM_REL + 1, H])
        ew_rr = sb("ew_rr", [NUM_REL + 1, H])
        biases = sb("biases", [3, H])
        bias_all = sb("bias_all", [KB, H], fp32r)
        bias_rhs = sb("bias_rhs", [KB, H], fp32r)

        x_in = [sb(f"x_in{s}", [P, G, H]) for s in range(2)]
        adj_in = [sb(f"adj_in{s}", [P, G, N], i32) for s in range(2)]
        a_r = [sb(f"a_r{s}", [P, G, N], fp32r) for s in range(2)]
        t_sum = [sb(f"t_sum{s}", [P, G, H]) for s in range(2)]
        y_out = [sb(f"y_out{s}", [P, G, H]) for s in range(2)]
        factors = [sb(f"factors{s}", [KB, G, N], fp32r) for s in range(2)]
        deg = [sb(f"deg{s}", [P, G]) for s in range(2)]
        inv_deg = [sb(f"inv_deg{s}", [P, G]) for s in range(2)]
        stats = [sb(f"stats{s}", [P, G, 6]) for s in range(2)]
        moments = [sb(f"moments{s}", [P, 5, G]) for s in range(2)]
        var_eps = [sb(f"var_eps{s}", [P, G]) for s in range(2)]
        root = [sb(f"root{s}", [P, G]) for s in range(2)]
        newton = [sb(f"newton{s}", [P, 4, G]) for s in range(2)]
        rstd = [sb(f"rstd{s}", [P, G]) for s in range(2)]
        shift = [sb(f"shift{s}", [P, G]) for s in range(2)]
        odd_scratch = sb("odd_scratch", [P, G, N])
        x_hi = [sb(f"x_hi{s}", [P, HC * N], fp32r) for s in range(2)]
        x_lo = [sb(f"x_lo{s}", [P, HC * N], fp32r) for s in range(2)]
        z_hi = [sb(f"z_hi{s}", [P, H], fp32r) for s in range(2)]
        z_lo = [sb(f"z_lo{s}", [P, H], fp32r) for s in range(2)]
        ctx_sb = [sb(f"ctx_sb{s}", [P, H]) for s in range(2)]
        resid = [sb(f"resid{s}", [P, H]) for s in range(2)]
        odd = sb("odd", [P, 2])
        odd_sum = sb("odd_sum", [P, 1])
        verdict = sb("verdict", [P, 1])
        flag = sb("flag", [1, 1], i32)
        gx = sb("gx", [P, H])
        gadj = sb("gadj", [P, N], i32)
        g_a = sb("g_a", [P, N])
        g_at = sb("g_at", [P, N])
        g_xt = sb("g_xt", [P, HC * N])
        g_idx = sb("g_idx", [P, 2, N])
        g_tmp = sb("g_tmp", [P, N])
        g_hot = sb("g_hot", [P, NUM_REL, N])
        g_cnt = [sb(f"g_cnt{s}", [P, NUM_REL + 1]) for s in range(2)]
        g_cnt_t = [sb(f"g_cnt_t{s}", [NUM_REL + 1, N]) for s in range(2)]
        g_inv = sb("g_inv", [P, 4])
        g_z = [sb(f"g_z{s}", [P, H]) for s in range(2)]
        g_t = sb("g_t", [P, H])
        g_stats = sb("g_stats", [P, 6])
        g_mv = sb("g_mv", [P, 5])
        g_ln = sb("g_ln", [P, 8])
        g_y = sb("g_y", [P, H])
        g_bias = sb("g_bias", [1, 3, H])

        banks = [ctx.enter_context(nc.psum_tensor(f"bank{i}", [P, 512], fp32)) for i in range(8)]
        ps_xt = banks[0]
        ps_chk = banks[1]
        ps_z = banks[2:4]
        ps_s = banks[4:6]
        ps_c = banks[6:8]

        table_in = sem("table_in")
        nb_w_in = sem("nb_w_in")
        self_w_in = sem("self_w_in")
        rel_w_in = sem("rel_w_in")
        x_loaded = [sem(f"x_loaded{s}") for s in range(2)]
        adj_loaded = [sem(f"adj_loaded{s}") for s in range(2)]
        stored = [sem(f"stored{s}") for s in range(2)]
        setup_dve = sem("setup_dve")
        nb_split = sem("nb_split")
        self_split = sem("self_split")
        self_hi_done = sem("self_hi_done")
        ones_ready = sem("ones_ready")
        ew_ready = sem("ew_ready")
        bias_summed = sem("bias_summed")
        bias_hi_done = sem("bias_hi_done")
        bias_ready = sem("bias_ready")
        xt_done = sem("xt_done")
        x_hi_done = sem("x_hi_done")
        x_lo_done = sem("x_lo_done")
        z_done = sem("z_done")
        z_hi_done = sem("z_hi_done")
        z_lo_done = sem("z_lo_done")
        c_done = sem("c_done")
        ctx_done = sem("ctx_done")
        resid_done = sem("resid_done")
        s_done = sem("s_done")
        t_done = sem("t_done")
        stats_done = sem("stats_done")
        y_done = sem("y_done")
        cast_done = sem("cast_done")
        at_done = sem("at_done")
        odd_done = sem("odd_done")
        odd_summed = sem("odd_summed")
        deg_row_done = sem("deg_row_done")
        factors_done = sem("factors_done")
        deg_done = sem("deg_done")
        deg_max_done = sem("deg_max_done")
        inv_deg_done = sem("inv_deg_done")
        moments_done = sem("moments_done")
        var_eps_done = sem("var_eps_done")
        root_done = sem("root_done")
        newton_done = sem("newton_done")
        rstd_done = sem("rstd_done")
        shift_done = sem("shift_done")
        verdict_steps = sem("verdict_steps")
        verdict_ready = sem("verdict_ready")
        verdict_summed = sem("verdict_summed")
        flag_ready = sem("flag_ready")
        g_loaded = sem("g_loaded")
        g_pe = sem("g_pe")
        g_dve = sem("g_dve")
        g_act = sem("g_act")
        g_stored = sem("g_stored")

        class At:

            def __init__(self, it, k):
                self.it, self.k = it, k
                self.fixed = isinstance(it, int)
                self.slot, self.j, self.gslot = k % 2, k % G, (k // G) % 2

            def __add__(self, n):
                return At(self.it, self.k + n)

            def exists(self):
                return not self.fixed or 0 <= UNROLL * self.it + self.k < B

            def graphs(self, n=0):
                return self.it * UNROLL + (self.k + 1 + n)

            def group(self, n=0):
                return self.it * (UNROLL // G) + (self.k // G + 1 + n)

            def group_exists(self, n=0):
                return not self.fixed or 0 <= self.it * (UNROLL // G) + self.k // G + n < NG

            def transfers(self, n=0):
                return self.it * 16 + 16 * ((self.k // G + n) // 2 + 1)

        def wait(eng, s, count):
            if not isinstance(count, int) or count > 0:
                eng.wait_ge(s, count)

        def run_steps(eng, step, first, last):
            for k in range(first, UNROLL):
                step(At(0, k))
            with eng.Fori(1, ITERS - 1) as it:
                for k in range(UNROLL):
                    step(At(it, k))
            for k in range(last + 1 - UNROLL * (ITERS - 1)):
                step(At(ITERS - 1, k))

        G_COUNTED, G_COPIED, G_VAR, G_DVE = 22, 26, 37, 43

        block = ctx.enter_context(nc.Block())

        @block.sync
        def _(sp):
            sp.dma_start(tab[:, :], table).then_inc(table_in, 16)
            for g in range(2):
                sp.dma_start(x_in[g][:, :, :], x_groups[g]).then_inc(x_loaded[g], 16)
                sp.dma_start(adj_in[g][:, :, :], adj_groups[g]).then_inc(adj_loaded[g], 16)

            def step(at):
                if at.j:
                    return
                s = at.gslot
                loads, stores = at.group_exists(2), at.group_exists(-1)
                to_load = at.group(1) if at.fixed else sp.snap(at.group(1))
                to_store = at.group(-2) if at.fixed else sp.snap(at.group(-2))
                if loads:
                    wait(sp, resid_done, at.graphs(G - 1))
                    sp.dma_start(x_in[s][:, :, :], dram(x_groups, to_load)).then_inc(x_loaded[s], 16)
                    wait(sp, cast_done, at.group())
                    wait(sp, deg_done, at.group())
                    sp.dma_start(adj_in[s][:, :, :], dram(adj_groups, to_load)).then_inc(adj_loaded[s], 16)
                if stores:
                    wait(sp, y_done, at.graphs(-1))
                    sp.dma_start(dram(out_groups, to_store), y_out[1 - s][:, :, :]).then_inc(stored[1 - s], 16)

            def dram(t, i):
                return t[i] if isinstance(i, int) else t[bass.ds(i, 1)].squeeze(0)

            run_steps(sp, step, 0, B)
            for s in range(2):
                sp.wait_ge(stored[s], 16 * NG // 2)
            sp.wait_ge(flag_ready, 1)
            with sp.If(sp.value_load(flag[0:1, 0:1], min_val=0, max_val=P) > 0):
                with sp.Fori(0, B) as b:
                    sp.wait_ge(g_stored, b * 16)
                    sp.dma_start(gx[:, :], x[bass.ds(b, 1)].squeeze(0)).then_inc(g_loaded, 16)
                    sp.dma_start(gadj[:, :], adj[bass.ds(b, 1)].squeeze(0)).then_inc(g_loaded, 16)
                    sp.wait_ge(g_dve, (b + 1) * G_DVE)
                    sp.dma_start(out[bass.ds(b, 1)].squeeze(0), g_y[:, :]).then_inc(g_stored, 16)
                sp.wait_ge(g_stored, B * 16)

        @block.tensor
        def _(pe):
            def products(bank, rhs_hi, rhs_lo, x_slot, more=None):
                terms = [(x_hi, rhs_hi), (x_hi, rhs_lo), (x_lo, rhs_hi)]
                for n, (lhs, rhs) in enumerate(terms):
                    if lhs is x_lo and more is not None:
                        more()
                    for c in range(HC):
                        last = nc.tensor.matmul(bank[:, 0:H], lhs[x_slot][:, c * N:(c + 1) * N], rhs[:, c, :],
                                                start=(n == 0 and c == 0), stop=(n == len(terms) - 1 and c == HC - 1))
                return last

            def step(at):
                g = at.gslot
                if at.exists():
                    wait(pe, x_hi_done, at.graphs())
                    wait(pe, z_lo_done, at.graphs(-2))
                    products(ps_z[at.slot], nb_hi, nb_lo, at.slot,
                             lambda: wait(pe, x_lo_done, at.graphs())).then_inc(z_done, 1)
                nxt = at + 1
                if nxt.exists():
                    if nxt.j == 0:
                        wait(pe, x_loaded[nxt.gslot], nxt.transfers())
                    wait(pe, x_lo_done, nxt.graphs(-1))
                    for c in range(HC):
                        last = nc.tensor.transpose(ps_xt[:, c * N:(c + 1) * N],
                                                   x_in[nxt.gslot][:, nxt.j, c * P:(c + 1) * P], ident)
                    last.then_inc(xt_done, 1)
                prev = at + -1
                if prev.exists():
                    wait(pe, z_hi_done, prev.graphs())
                    wait(pe, ctx_done, prev.graphs(-2))
                    a = a_r[prev.gslot][:, prev.j, :]
                    nc.tensor.matmul(ps_c[prev.slot][:, 0:H], a, z_hi[prev.slot][:, :], start=True, stop=False)
                    wait(pe, z_lo_done, prev.graphs())
                    nc.tensor.matmul(ps_c[prev.slot][:, 0:H], a, z_lo[prev.slot][:, :],
                                     start=False, stop=True).then_inc(c_done, 1)
                if at.j == 0 and at.group_exists():
                    wait(pe, factors_done, at.group())
                    for j in range(G):
                        last = nc.tensor.transpose(ps_chk[:, j * N:(j + 1) * N], a_r[g][:, j, :].bitcast(fp32), ident)
                    last.then_inc(at_done, 1)
                if at.j == 2 and at.group_exists(1):
                    wait(pe, cast_done, at.group(1))
                    wait(pe, odd_done, at.group())
                    nc.tensor.matmul(ps_chk[:, :], ones_r[:, :], a_r[1 - g][:, :, :],
                                     start=True, stop=True).then_inc(deg_row_done, 1)
                if at.exists():
                    wait(pe, t_done, at.graphs(-2))
                    if at.j == 0:
                        wait(pe, factors_done, at.group())
                    bank = ps_s[at.slot]
                    nc.tensor.matmul(bank[:, 0:H], factors[g][:, at.j, :], bias_rhs[:, :], start=True, stop=False)
                    for n, (lhs, rhs) in enumerate([(x_hi, self_hi), (x_hi, self_lo), (x_lo, self_hi)]):
                        for c in range(HC):
                            last = nc.tensor.matmul(bank[:, 0:H], lhs[at.slot][:, c * N:(c + 1) * N], rhs[:, c, :],
                                                    start=False, stop=(n == 2 and c == HC - 1))
                    last.then_inc(s_done, 1)

            pe.wait_ge(rel_w_in, 16 * 10)
            nc.tensor.matmul(ps_z[0][0:NUM_REL, 0:H], e_t[:, :], wr_t[:, :], start=True, stop=True)
            nc.tensor.matmul(ps_z[1][0:NUM_REL, 0:H], e_t[:, :], wrr_t[:, :],
                             start=True, stop=True).then_inc(setup_dve, 1)
            pe.wait_ge(ew_ready, 2)
            pe.wait_ge(table_in, 16)
            nc.tensor.matmul(ps_s[0][0:KB, 0:H], tab[0:NUM_REL + 1, C_SEL_R:C_SEL_R + KB], ew_r[:, :],
                             start=True, stop=False)
            nc.tensor.matmul(ps_s[0][0:KB, 0:H], tab[0:NUM_REL + 1, C_SEL_RR:C_SEL_RR + KB], ew_rr[:, :],
                             start=False, stop=False)
            nc.tensor.matmul(ps_s[0][0:KB, 0:H], tab[0:3, C_SEL_B:C_SEL_B + KB], biases[:, :],
                             start=False, stop=True).then_inc(bias_summed, 1)
            pe.wait_ge(ones_ready, 1)
            pe.wait_ge(bias_ready, 2)
            pe.wait_ge(nb_split, 2)
            pe.wait_ge(self_split, 1)
            run_steps(pe, step, -2, B)

            pe.wait_ge(verdict_ready, 1)
            nc.tensor.matmul(ps_chk[0:1, 0:1], verdict[:, 0:1], tab[:, C_ONE:C_ONE + 1],
                             start=True, stop=True).then_inc(verdict_summed, 1)
            pe.wait_ge(flag_ready, 1)
            with pe.If(pe.value_load(flag[0:1, 0:1], min_val=0, max_val=P) > 0):
                with pe.Fori(0, B) as b:
                    pe.wait_ge(g_loaded, (b + 1) * 32)
                    pe.wait_ge(g_dve, b * G_DVE + 1)
                    for c in range(HC):
                        nc.tensor.transpose(banks[0][:, c * N:(c + 1) * N], gx[:, c * P:(c + 1) * P], ident)
                    nc.tensor.transpose(banks[1][:, 0:N], g_a[:, :], ident).then_inc(g_pe, 1)
                    pe.wait_ge(g_dve, b * G_DVE + G_COUNTED)
                    for s in range(2):
                        nc.tensor.transpose(banks[2 + s][0:NUM_REL + 1, 0:N], g_cnt[s][:, :], ident)
                    for s, w in enumerate((w_adj, w_rev)):
                        for c in range(HC):
                            nc.tensor.matmul(banks[4 + s][:, 0:H], g_xt[:, c * N:(c + 1) * N], w[:, c, :],
                                             start=(c == 0), stop=False)
                        last = nc.tensor.matmul(banks[4 + s][:, 0:H], tab[0:1, C_ONE:C_ONE + P], g_bias[:, s, :],
                                                start=False, stop=True)
                    last.then_inc(g_pe, 1)
                    pe.wait_ge(g_dve, b * G_DVE + G_COPIED)
                    nc.tensor.matmul(banks[6][:, 0:H], g_at[:, :], g_z[0][:, :], start=True, stop=True)
                    nc.tensor.matmul(banks[7][:, 0:H], g_a[:, :], g_z[1][:, :], start=True, stop=True)
                    for c in range(HC):
                        nc.tensor.matmul(banks[0][:, 0:H], g_xt[:, c * N:(c + 1) * N], w_self[:, c, :],
                                         start=(c == 0), stop=False)
                    nc.tensor.matmul(banks[0][:, 0:H], tab[0:1, C_ONE:C_ONE + P], g_bias[:, 2, :],
                                     start=False, stop=False)
                    nc.tensor.matmul(banks[0][:, 0:H], g_cnt_t[0][:, :], ew_r[:, :], start=False, stop=False)
                    nc.tensor.matmul(banks[0][:, 0:H], g_cnt_t[1][:, :], ew_rr[:, :],
                                     start=False, stop=True).then_inc(g_pe, 1)

        @block.scalar
        def _(act):
            act.dma_start(w_adj[:, :, :], WadjT.rearrange("(c p) o -> p c o", p=P)).then_inc(nb_w_in, 16)
            act.dma_start(w_rev[:, :, :], WrevT.rearrange("(c p) o -> p c o", p=P)).then_inc(nb_w_in, 16)
            for dst, src in ((e_t[:, :], ET), (wr_t[:, :], WrT), (wrr_t[:, :], WrrT),
                             (ew_r[NUM_REL:NUM_REL + 1, :], br), (ew_rr[NUM_REL:NUM_REL + 1, :], brr),
                             (biases[0:1, :], badj), (biases[1:2, :], brev), (biases[2:3, :], bself)):
                act.dma_start(dst, src).then_inc(rel_w_in, 16)
            for s, src in enumerate((badj, brev)):
                act.dma_start(g_bias[:, s, :], src).then_inc(rel_w_in, 16)
            act.dma_start(g_bias[:, 2, :], bself).then_inc(self_w_in, 16)
            act.dma_start(w_self[:, :, :], WselfT.rearrange("(c p) o -> p c o", p=P)).then_inc(self_w_in, 16)
            act.wait_ge(bias_summed, 1)
            nc.scalar.copy(bias_all[:, :], ps_s[0][0:KB, 0:H]).then_inc(bias_hi_done, 1)
            act.wait_ge(self_w_in, 32)
            nc.scalar.copy(self_hi[:, :, :], w_self[:, :, :]).then_inc(self_hi_done, 1)

            def step(at):
                done = at + -NORM_LAG
                if done.exists():
                    if done.j == 0:
                        wait(act, rstd_done, done.group())
                        wait(act, shift_done, done.group())
                        wait(act, stored[done.gslot], done.transfers(-2))
                    nc.scalar.activation(y_out[done.gslot][:, done.j, :], t_sum[done.gslot][:, done.j, :],
                                         ACT.Identity, bias=shift[done.gslot][:, done.j:done.j + 1],
                                         scale=rstd[done.gslot][:, done.j:done.j + 1]).then_inc(y_done, 1)
                if at.j == 2 and at.group_exists(-1):
                    s = 1 - at.gslot
                    wait(act, var_eps_done, at.group(-1))
                    nc.scalar.activation(root[s][:, :], var_eps[s][:, :], ACT.Sqrt).then_inc(root_done, 1)
                if at.exists():
                    wait(act, z_done, at.graphs())
                    wait(act, c_done, at.graphs(-2))
                    nc.scalar.copy(z_hi[at.slot][:, :], ps_z[at.slot][:, 0:H]).then_inc(z_hi_done, 1)
                nxt = at + 1
                if nxt.exists():
                    wait(act, xt_done, nxt.graphs())
                    wait(act, s_done, nxt.graphs(-2))
                    nc.scalar.copy(x_hi[nxt.slot][:, :], ps_xt[:, 0:HC * N]).then_inc(x_hi_done, 1)
                prev = at + -1
                if prev.exists():
                    wait(act, c_done, prev.graphs())
                    if prev.j == 0:
                        wait(act, inv_deg_done, prev.group())
                    wait(act, resid_done, prev.graphs(-2))
                    nc.scalar.activation(ctx_sb[prev.slot][:, :], ps_c[prev.slot][:, 0:H], ACT.Copy,
                                         scale=inv_deg[prev.gslot][:, prev.j:prev.j + 1]).then_inc(ctx_done, 1)

            run_steps(act, step, -1, B - 1 + NORM_LAG)
            act.wait_ge(flag_ready, 1)
            with act.If(act.value_load(flag[0:1, 0:1], min_val=0, max_val=P) > 0):
                with act.Fori(0, B) as b:
                    act.wait_ge(g_dve, b * G_DVE + G_VAR)
                    nc.scalar.activation(g_ln[:, 1:2], g_ln[:, 0:1], ACT.Sqrt).then_inc(g_act, 1)

        @block.gpsimd
        def _(pool):
            def step(at):
                cast = at.j == 1 and at.group_exists(1)
                s, nxt, prev = 1 - at.gslot, at + G, at + -1
                if cast:
                    wait(pool, adj_loaded[s], nxt.transfers())
                    wait(pool, c_done, at.graphs(-2))
                    wait(pool, odd_done, at.group(-1))
                if prev.exists():
                    wait(pool, t_done, prev.graphs(-2))
                    wait(pool, ctx_done, prev.graphs())
                    nc.gpsimd.tensor_tensor(resid[prev.slot][:, :], ctx_sb[prev.slot][:, :],
                                            x_in[prev.gslot][:, prev.j, :], ALU.add).then_inc(resid_done, 1)
                if cast:
                    nc.gpsimd.tensor_copy(a_r[s][:, :, :], adj_in[s][:, :, :]).then_inc(cast_done, 1)

            run_steps(pool, step, -3, B)

        def general(dve, b):
            n = [0]

            def link(ins):
                ins.then_inc(g_dve, 1)
                n[0] += 1
                dve.wait_ge(g_dve, b * G_DVE + n[0])

            def v(*a, **k):
                link(nc.vector.tensor_scalar(*a, **k))

            dve.wait_ge(g_loaded, (b + 1) * 32)
            link(nc.vector.tensor_copy(g_a[:, :], gadj[:, :]))
            dve.wait_ge(g_pe, b * 3 + 1)
            link(nc.vector.tensor_copy(g_xt[:, :], banks[0][:, 0:HC * N]))
            link(nc.vector.tensor_copy(g_at[:, :], banks[1][:, 0:N]))
            v(g_tmp[:, :], g_a[:, :], 0.0, float(NUM_REL), ALU.is_lt, ALU.mult)
            link(nc.vector.tensor_tensor(g_tmp[:, :], g_tmp[:, :], g_a[:, :], ALU.add))
            v(g_idx[:, 0, :], g_tmp[:, :], 0.0, float(NUM_REL - 1), ALU.max, ALU.min)
            v(g_tmp[:, :], g_at[:, :], float(NUM_BASE), float(NUM_REL - 1), ALU.add, ALU.min)
            v(g_idx[:, 1, :], g_at[:, :], 0.0, None, ALU.is_gt)
            link(nc.vector.tensor_tensor(g_idx[:, 1, :], g_idx[:, 1, :], g_tmp[:, :], ALU.mult))
            for s, a in enumerate((g_a, g_at)):
                def over_c(t):
                    return t.unsqueeze(1).to_broadcast([P, NUM_REL, N])
                iota = tab[:, C_IOTA:C_IOTA + NUM_REL].unsqueeze(2).to_broadcast([P, NUM_REL, N])
                link(nc.vector.tensor_tensor(g_hot[:, :, :], over_c(g_idx[:, s, :]), iota, ALU.is_equal))
                link(nc.vector.tensor_tensor(g_hot[:, :, :], g_hot[:, :, :], over_c(a[:, :]), ALU.mult))
                link(nc.vector.tensor_reduce(g_cnt[s][:, 0:NUM_REL], g_hot[:, :, :], AX.X, ALU.add))
                link(nc.vector.tensor_reduce(g_cnt[s][:, NUM_REL:NUM_REL + 1], a[:, :], AX.X, ALU.add))
                d = g_cnt[s][:, NUM_REL:NUM_REL + 1]
                v(g_inv[:, s:s + 1], d, 0.0, None, ALU.is_le)
                link(nc.vector.scalar_tensor_tensor(out=g_inv[:, 2 + s:3 + s], in0=d, scalar=0.0,
                                                    in1=g_inv[:, s:s + 1], op0=ALU.max, op1=ALU.add))
            link(nc.vector.reciprocal(g_inv[:, 0:2], g_inv[:, 2:4]))
            assert n[0] == G_COUNTED
            dve.wait_ge(g_pe, b * 3 + 2)
            for s in range(2):
                link(nc.vector.tensor_copy(g_cnt_t[s][:, :], banks[2 + s][0:NUM_REL + 1, 0:N]))
                link(nc.vector.tensor_copy(g_z[s][:, :], banks[4 + s][:, 0:H]))
            assert n[0] == G_COPIED
            dve.wait_ge(g_pe, b * 3 + 3)
            for s, more in enumerate((gx, g_t)):
                link(nc.vector.scalar_tensor_tensor(out=g_t[:, :], in0=banks[6 + s][:, 0:H],
                                                    scalar=g_inv[:, s:s + 1], in1=more[:, :],
                                                    op0=ALU.mult, op1=ALU.add))
            link(nc.vector.tensor_tensor(g_t[:, :], banks[0][:, 0:H], g_t[:, :], ALU.add))
            link(nc.vector.bn_stats(g_stats[:, :], g_t[:, :]))
            st, m = g_stats, g_mv
            link(nc.vector.tensor_tensor(m[:, 0:1], st[:, 1:2], st[:, 4:5], ALU.add))
            v(m[:, 0:1], m[:, 0:1], 0.5, None, ALU.mult)
            link(nc.vector.tensor_tensor(m[:, 1:2], st[:, 1:2], st[:, 4:5], ALU.subtract))
            link(nc.vector.tensor_tensor(m[:, 2:3], m[:, 1:2], m[:, 1:2], ALU.mult))
            link(nc.vector.tensor_tensor(m[:, 3:4], st[:, 2:3], st[:, 5:6], ALU.add))
            v(m[:, 4:5], m[:, 3:4], 1.0 / H, EPS, ALU.mult, ALU.add)
            link(nc.vector.scalar_tensor_tensor(out=g_ln[:, 0:1], in0=m[:, 2:3], scalar=0.25, in1=m[:, 4:5],
                                                op0=ALU.mult, op1=ALU.add))
            assert n[0] == G_VAR
            dve.wait_ge(g_act, b + 1)
            link(nc.vector.reciprocal(g_ln[:, 2:3], g_ln[:, 1:2]))
            link(nc.vector.tensor_tensor(g_ln[:, 3:4], g_ln[:, 2:3], g_ln[:, 2:3], ALU.mult))
            link(nc.vector.tensor_tensor(g_ln[:, 4:5], g_ln[:, 3:4], g_ln[:, 0:1], ALU.mult))
            v(g_ln[:, 5:6], g_ln[:, 4:5], -0.5, 1.5, ALU.mult, ALU.add)
            link(nc.vector.tensor_tensor(g_ln[:, 6:7], g_ln[:, 5:6], g_ln[:, 2:3], ALU.mult))
            v(g_y[:, :], g_t[:, :], g_mv[:, 0:1], g_ln[:, 6:7], ALU.subtract, ALU.mult)
            assert n[0] == G_DVE

        @block.vector
        def _(dve):
            nc.vector.memset(odd_sum[:, :], 0.0).then_inc(verdict_steps, 1)
            dve.wait_ge(table_in, 16)
            nc.vector.tensor_copy(ones_r[:, :], tab[:, C_ONE:C_ONE + P]).then_inc(ones_ready, 1)
            dve.wait_ge(nb_w_in, 32)
            nc.vector.tensor_tensor(w_nb[:, :, :], w_adj[:, :, :], w_rev[:, :, :], ALU.add).then_inc(verdict_steps, 1)
            dve.wait_ge(verdict_steps, 2)
            nc.vector.tensor_copy(nb_hi[:, :, :], w_nb[:, :, :]).then_inc(nb_split, 1)
            dve.wait_ge(nb_split, 1)
            nc.vector.tensor_tensor(nb_lo[:, :, :], w_nb[:, :, :], nb_hi[:, :, :].bitcast(fp32),
                                    ALU.subtract).then_inc(nb_split, 1)
            dve.wait_ge(setup_dve, 1)
            nc.vector.tensor_copy(ew_r[0:NUM_REL, :], ps_z[0][0:NUM_REL, 0:H]).then_inc(ew_ready, 1)
            nc.vector.tensor_copy(ew_rr[0:NUM_REL, :], ps_z[1][0:NUM_REL, 0:H]).then_inc(ew_ready, 1)
            dve.wait_ge(bias_hi_done, 1)
            nc.vector.tensor_copy(bias_rhs[0:LOW, :], bias_all[0:LOW, :].bitcast(fp32)).then_inc(bias_ready, 1)
            nc.vector.tensor_tensor(bias_rhs[LOW:KB, :], ps_s[0][LOW:KB, 0:H], bias_all[LOW:KB, :].bitcast(fp32),
                                    ALU.subtract).then_inc(bias_ready, 1)
            dve.wait_ge(self_hi_done, 1)
            nc.vector.tensor_tensor(self_lo[:, :, :], w_self[:, :, :], self_hi[:, :, :].bitcast(fp32),
                                    ALU.subtract).then_inc(self_split, 1)

            def step(at):
                old = at + -2
                if old.exists():
                    s = old.gslot
                    wait(dve, resid_done, old.graphs())
                    wait(dve, s_done, old.graphs())
                    wait(dve, y_done, old.graphs(-UNROLL - min(old.k, 0)))
                    nc.vector.tensor_tensor(t_sum[s][:, old.j, :], ps_s[old.slot][:, 0:H], resid[old.slot][:, :],
                                            ALU.add).then_inc(t_done, 1)
                if at.exists():
                    wait(dve, z_hi_done, at.graphs())
                    nc.vector.tensor_tensor(z_lo[at.slot][:, :], ps_z[at.slot][:, 0:H],
                                            z_hi[at.slot][:, :].bitcast(fp32), ALU.subtract).then_inc(z_lo_done, 1)
                nxt = at + 1
                if nxt.exists():
                    wait(dve, x_hi_done, nxt.graphs())
                    wait(dve, s_done, nxt.graphs(-2))
                    nc.vector.tensor_tensor(x_lo[nxt.slot][:, :], ps_xt[:, 0:HC * N],
                                            x_hi[nxt.slot][:, :].bitcast(fp32), ALU.subtract).then_inc(x_lo_done, 1)
                if old.exists():
                    wait(dve, t_done, old.graphs())
                    nc.vector.bn_stats(stats[old.gslot][:, old.j, :],
                                       t_sum[old.gslot][:, old.j, :]).then_inc(stats_done, 1)
                if at.j == 0 and at.group_exists():
                    s = at.gslot
                    wait(dve, at_done, at.group())
                    nc.vector.scalar_tensor_tensor(out=odd_scratch[:, :, :],
                                                   in0=ps_chk[:, :].rearrange("p (j n) -> p j n", j=G), scalar=0.0,
                                                   in1=a_r[s][:, :, :].bitcast(fp32), op0=ALU.is_gt,
                                                   op1=ALU.not_equal, accum_out=odd[:, s:s + 1]).then_inc(odd_done, 1)
                    wait(dve, odd_done, at.group())
                    wait(dve, odd_summed, at.group(-1))
                    nc.vector.tensor_tensor(odd_sum[:, :], odd_sum[:, :], odd[:, s:s + 1],
                                            ALU.add).then_inc(odd_summed, 1)
                if at.j == 1 and at.group_exists(-1):
                    s = 1 - at.gslot
                    wait(dve, stats_done, at.graphs(-2))
                    m, st, steps = moments[s], stats[s], 5 * at.group(-1)
                    nc.vector.tensor_tensor(m[:, 0, :], st[:, :, 1], st[:, :, 4], ALU.add).then_inc(moments_done, 1)
                    nc.vector.tensor_tensor(m[:, 1, :], st[:, :, 1], st[:, :, 4], ALU.subtract).then_inc(moments_done, 1)
                    nc.vector.tensor_tensor(m[:, 2, :], st[:, :, 2], st[:, :, 5], ALU.add).then_inc(moments_done, 1)
                    wait(dve, moments_done, steps - 3)
                    nc.vector.tensor_tensor(m[:, 3, :], m[:, 1, :], m[:, 1, :], ALU.mult).then_inc(moments_done, 1)
                    wait(dve, moments_done, steps - 2)
                    nc.vector.tensor_scalar(m[:, 4, :], m[:, 2, :], 1.0 / H, EPS, ALU.mult, ALU.add).then_inc(moments_done, 1)
                    wait(dve, moments_done, steps)
                    nc.vector.scalar_tensor_tensor(out=var_eps[s][:, :], in0=m[:, 3, :], scalar=0.25, in1=m[:, 4, :],
                                                   op0=ALU.mult, op1=ALU.add).then_inc(var_eps_done, 1)
                if at.j == 2 and at.group_exists(-1):
                    s = 1 - at.gslot
                    w, steps = newton[s], 4 * at.group(-1)
                    wait(dve, root_done, at.group(-1))
                    nc.vector.reciprocal(w[:, 0, :], root[s][:, :]).then_inc(newton_done, 1)
                    wait(dve, newton_done, steps - 3)
                    nc.vector.tensor_tensor(w[:, 1, :], w[:, 0, :], w[:, 0, :], ALU.mult).then_inc(newton_done, 1)
                    wait(dve, newton_done, steps - 2)
                    nc.vector.tensor_tensor(w[:, 2, :], w[:, 1, :], var_eps[s][:, :], ALU.mult).then_inc(newton_done, 1)
                    wait(dve, newton_done, steps - 1)
                    nc.vector.tensor_scalar(w[:, 3, :], w[:, 2, :], -0.5, 1.5, ALU.mult, ALU.add).then_inc(newton_done, 1)
                    wait(dve, newton_done, steps)
                    nc.vector.tensor_tensor(rstd[s][:, :], w[:, 3, :], w[:, 0, :], ALU.mult).then_inc(rstd_done, 1)
                    wait(dve, rstd_done, at.group(-1))
                    nc.vector.scalar_tensor_tensor(out=shift[s][:, :], in0=moments[s][:, 0, :], scalar=-0.5,
                                                   in1=rstd[s][:, :], op0=ALU.mult, op1=ALU.mult).then_inc(shift_done, 1)
                if at.j == 3 and at.group_exists(1):
                    s = 1 - at.gslot
                    wait(dve, adj_loaded[s], (at + G).transfers())
                    nc.vector.tensor_reduce(deg[s][:, :], adj_in[s][:, :, :], AX.X, ALU.add).then_inc(deg_done, 1)
                    wait(dve, deg_row_done, at.group(1))
                    wait(dve, s_done, at.graphs(-G))
                    nc.vector.tensor_scalar(factors[s][:, :, :], ps_chk[0:KB, :].rearrange("p (j n) -> p j n", j=G),
                                            tab[0:KB, C_LIM:C_LIM + 1], tab[0:KB, C_LIM + 1:C_LIM + 2],
                                            ALU.max, ALU.min).then_inc(factors_done, 1)
                    wait(dve, deg_done, at.group(1))
                    nc.vector.tensor_scalar(deg[s][:, :], deg[s][:, :], 1.0, None, ALU.max).then_inc(deg_max_done, 1)
                    wait(dve, deg_max_done, at.group(1))
                    wait(dve, ctx_done, at.graphs(-G))
                    nc.vector.reciprocal(inv_deg[s][:, :], deg[s][:, :]).then_inc(inv_deg_done, 1)

            run_steps(dve, step, -2, B + 2)

            dve.wait_ge(odd_summed, NG)
            nc.vector.tensor_scalar(verdict[:, :], odd_sum[:, :], 0.0, None, ALU.is_gt).then_inc(verdict_ready, 1)
            dve.wait_ge(verdict_summed, 1)
            nc.vector.tensor_copy(flag[:, :], ps_chk[0:1, 0:1]).then_inc(flag_ready, 1)
            dve.wait_ge(flag_ready, 1)
            with dve.If(dve.value_load(flag[0:1, 0:1], min_val=0, max_val=P) > 0):
                with dve.Fori(0, B) as b:
                    general(dve, b)


def kernel(x, adj, L0_gnn_E, L0_gnn_Wadj, L0_gnn_badj, L0_gnn_Wrev, L0_gnn_brev, L0_gnn_Wself, L0_gnn_bself,
           L0_gnn_Wr, L0_gnn_br, L0_gnn_Wrr, L0_gnn_brr):
    import numpy as np
    import concourse.bacc as bacc
    from concourse.bass_utils import run_bass_kernel_spmd

    arrays = {"x": x, "adj": adj}
    for name, a in (("E", L0_gnn_E), ("Wadj", L0_gnn_Wadj), ("Wrev", L0_gnn_Wrev), ("Wself", L0_gnn_Wself),
                    ("Wr", L0_gnn_Wr), ("Wrr", L0_gnn_Wrr)):
        arrays[name + "T"] = np.asarray(a).T
    for name, a in (("badj", L0_gnn_badj), ("brev", L0_gnn_brev), ("bself", L0_gnn_bself),
                    ("br", L0_gnn_br), ("brr", L0_gnn_brr)):
        arrays[name] = np.asarray(a).reshape(1, H)
    arrays["table"] = constants()

    nc = bacc.Bacc("TRN2", target_bir_lowering=False, num_devices=1)
    arrays = {name: np.ascontiguousarray(a) for name, a in arrays.items()}
    tensors = {name: nc.dram_tensor(name, a.shape, mybir.dt.from_np(a.dtype), kind="ExternalInput").ap()
               for name, a in arrays.items()}
    out = nc.dram_tensor("out", (B, N, H), fp32, kind="ExternalOutput").ap()
    graph_layer(nc, out=out, **tensors)
    return run_bass_kernel_spmd(nc, [arrays], core_ids=[0]).results[0]["out"]
```

```python
from contextlib import ExitStack

import concourse.bass as bass
from concourse import mybir

fp32 = mybir.dt.float32
fp32r = mybir.dt.float32r
i32 = mybir.dt.int32
ALU = mybir.AluOpType
ACT = mybir.ActivationFunctionType
AX = mybir.AxisListType

B, N, H = 64, 128, 384
R = 128
NUM_REL, NUM_BASE = 80, 40
P = 128
HC = H // P
G = 4
NG = B // G
UNROLL = 2 * G
ITERS = B // UNROLL
EPS = 1e-5
NORM_LAG = 7
KB = 64
LOW = 32

C_ID = 0
C_SEL = C_ID + P
C_LIM = C_SEL + KB
C_END = C_LIM + 2
R_E, R_WR, R_WRR, R_END = 0, NUM_REL, NUM_REL + H, NUM_REL + 2 * H
B_ADJ, B_REV, B_SELF, B_R, B_RR = range(5)


def constants():
    import numpy as np

    t = np.zeros((P, C_END), np.float32)
    t[:, C_ID:C_ID + P] = np.eye(P)
    for m in (0, LOW):
        t[[B_R, B_RR], C_SEL + m] = 1.0
        t[B_SELF, C_SEL + m + 1] = 1.0
        t[[B_ADJ, B_REV], C_SEL + m + 2] = 1.0
        t[m, C_LIM:C_LIM + 2] = 0.0, N
        t[m + 1, C_LIM:C_LIM + 2] = 1.0, 1.0
        t[m + 2, C_LIM:C_LIM + 2] = 0.0, 1.0
    return t, np.tile(np.arange(NUM_REL, dtype=np.float32), (P, 1))


def graph_layer(nc, x, adj, WadjT, WrevT, WselfT, rel_weights, bias_rows, table, count_to_80, out):
    x_groups = x.rearrange("(g e) i h -> g i e h", e=G)
    adj_groups = adj.rearrange("(g e) i j -> g i e j", e=G)
    out_groups = out.rearrange("(g e) i h -> g i e h", e=G)

    with ExitStack() as ctx:
        def sb(name, shape, dt=fp32):
            return ctx.enter_context(nc.sbuf_tensor(name, shape, dt))

        def sem(name):
            return ctx.enter_context(nc.semaphore(name))

        tab = sb("tab", [P, C_END])
        ident = tab[:, C_ID:C_ID + P]
        ones = sb("ones", [P, P])
        ones_r = sb("ones_r", [P, P], fp32r)
        ident_r = sb("ident_r", [P, P], fp32r)
        w_adj = sb("w_adj", [P, HC, H])
        w_rev = sb("w_rev", [P, HC, H])
        w_self = sb("w_self", [P, HC, H])
        w_nb = sb("w_nb", [P, HC, H])
        nb_hi = sb("nb_hi", [P, HC, H], fp32r)
        nb_lo = sb("nb_lo", [P, HC, H], fp32r)
        self_hi = sb("self_hi", [P, HC, H], fp32r)
        self_lo = sb("self_lo", [P, HC, H], fp32r)
        rel = sb("rel", [R, R_END])
        e_sel = sb("e_sel", [R, 2, KB])
        biases = sb("biases", [5, H])
        bias_all = sb("bias_all", [KB, H], fp32r)
        bias_rhs = sb("bias_rhs", [KB, H], fp32r)

        x_in = [sb(f"x_in{s}", [P, G, H]) for s in range(2)]
        adj_in = [sb(f"adj_in{s}", [P, G, N], i32) for s in range(2)]
        a_r = [sb(f"a_r{s}", [P, G, N], fp32r) for s in range(2)]
        t_sum = [sb(f"t_sum{s}", [P, G, H]) for s in range(2)]
        y_out = [sb(f"y_out{s}", [P, G, H]) for s in range(2)]
        factors = [sb(f"factors{s}", [KB, G, N], fp32r) for s in range(2)]
        deg = [sb(f"deg{s}", [P, G]) for s in range(2)]
        inv_deg = [sb(f"inv_deg{s}", [P, G]) for s in range(2)]
        stats = [sb(f"stats{s}", [P, G, 6]) for s in range(2)]
        moments = [sb(f"moments{s}", [P, 5, G]) for s in range(2)]
        var_eps = [sb(f"var_eps{s}", [P, G]) for s in range(2)]
        root = [sb(f"root{s}", [P, G]) for s in range(2)]
        newton = [sb(f"newton{s}", [P, 4, G]) for s in range(2)]
        rstd = [sb(f"rstd{s}", [P, G]) for s in range(2)]
        shift = [sb(f"shift{s}", [P, G]) for s in range(2)]
        odd_scratch = sb("odd_scratch", [P, G, N])
        x_hi = [sb(f"x_hi{s}", [P, HC * N], fp32r) for s in range(2)]
        x_lo = [sb(f"x_lo{s}", [P, HC * N], fp32r) for s in range(2)]
        z_hi = [sb(f"z_hi{s}", [P, H], fp32r) for s in range(2)]
        z_lo = [sb(f"z_lo{s}", [P, H], fp32r) for s in range(2)]
        ctx_sb = [sb(f"ctx_sb{s}", [P, H]) for s in range(2)]
        resid = [sb(f"resid{s}", [P, H]) for s in range(2)]
        odd = sb("odd", [P, 2])
        odd_sum = sb("odd_sum", [P, 1])
        verdict = sb("verdict", [P, 1])
        flag = sb("flag", [1, 1], i32)
        gx = sb("gx", [P, H])
        gadj = sb("gadj", [P, N], i32)
        g_a = sb("g_a", [P, N])
        g_at = sb("g_at", [P, N])
        g_xt = sb("g_xt", [P, HC * N])
        g_idx = sb("g_idx", [P, 2, N])
        g_tmp = sb("g_tmp", [P, N])
        g_hot = sb("g_hot", [P, NUM_REL, N])
        g_cnt = [sb(f"g_cnt{s}", [P, NUM_REL + 1]) for s in range(2)]
        g_cnt_t = [sb(f"g_cnt_t{s}", [NUM_REL + 1, N]) for s in range(2)]
        g_inv = sb("g_inv", [P, 4])
        g_z = [sb(f"g_z{s}", [P, H]) for s in range(2)]
        g_t = sb("g_t", [P, H])
        g_stats = sb("g_stats", [P, 6])
        g_mv = sb("g_mv", [P, 5])
        g_ln = sb("g_ln", [P, 8])
        g_y = sb("g_y", [P, H])
        g_bias = sb("g_bias", [1, 3, H])
        g_iota = sb("g_iota", [P, NUM_REL])
        ew_r = sb("ew_r", [NUM_REL + 1, H])
        ew_rr = sb("ew_rr", [NUM_REL + 1, H])

        banks = [ctx.enter_context(nc.psum_tensor(f"bank{i}", [P, 512], fp32)) for i in range(8)]
        ps_xt = banks[0]
        ps_chk = banks[1]
        ps_z = banks[2:4]
        ps_s = banks[4:6]
        ps_c = banks[6:8]

        table_in = sem("table_in")
        nb_w_in = sem("nb_w_in")
        self_w_in = sem("self_w_in")
        rel_in = sem("rel_in")
        first_x_loaded = sem("first_x_loaded")
        x_loaded = [sem(f"x_loaded{s}") for s in range(2)]
        adj_loaded = [sem(f"adj_loaded{s}") for s in range(2)]
        stored = [sem(f"stored{s}") for s in range(2)]
        nb_sum_done = sem("nb_sum_done")
        nb_hi_done = sem("nb_hi_done")
        nb_lo_done = sem("nb_lo_done")
        self_hi_done = sem("self_hi_done")
        self_lo_done = sem("self_lo_done")
        consts_ready = sem("consts_ready")
        e_sel_zero = sem("e_sel_zero")
        e_sel_ready = sem("e_sel_ready")
        bias_summed = sem("bias_summed")
        bias_hi_done = sem("bias_hi_done")
        bias_ready = sem("bias_ready")
        xt_done = sem("xt_done")
        x_hi_done = sem("x_hi_done")
        x_lo_done = sem("x_lo_done")
        z_done = sem("z_done")
        z_hi_done = sem("z_hi_done")
        z_lo_done = sem("z_lo_done")
        c_done = sem("c_done")
        ctx_done = sem("ctx_done")
        resid_done = sem("resid_done")
        s_done = sem("s_done")
        t_done = sem("t_done")
        stats_done = sem("stats_done")
        y_done = sem("y_done")
        cast_done = sem("cast_done")
        at_done = sem("at_done")
        odd_done = sem("odd_done")
        odd_summed = sem("odd_summed")
        deg_row_done = sem("deg_row_done")
        factors_done = sem("factors_done")
        deg_done = sem("deg_done")
        deg_max_done = sem("deg_max_done")
        inv_deg_done = sem("inv_deg_done")
        moments_done = sem("moments_done")
        var_eps_done = sem("var_eps_done")
        root_done = sem("root_done")
        newton_done = sem("newton_done")
        rstd_done = sem("rstd_done")
        shift_done = sem("shift_done")
        odd_cleared = sem("odd_cleared")
        verdict_ready = sem("verdict_ready")
        verdict_summed = sem("verdict_summed")
        flag_ready = sem("flag_ready")
        g_moved = sem("g_moved")
        g_setup_pe = sem("g_setup_pe")
        g_setup_dve = sem("g_setup_dve")
        last_stored = sem("last_stored")
        g_loaded = sem("g_loaded")
        g_pe = sem("g_pe")
        g_dve = sem("g_dve")
        g_act = sem("g_act")

        class At:

            def __init__(self, it, k):
                self.it, self.k = it, k
                self.fixed = isinstance(it, int)
                self.slot, self.j, self.gslot = k % 2, k % G, (k // G) % 2

            def __add__(self, n):
                return At(self.it, self.k + n)

            def exists(self):
                return not self.fixed or 0 <= UNROLL * self.it + self.k < B

            def is_graph(self, b):
                return self.fixed and UNROLL * self.it + self.k == b

            def graphs(self, n=0):
                return self.it * UNROLL + (self.k + 1 + n)

            def group(self, n=0):
                return self.it * (UNROLL // G) + (self.k // G + 1 + n)

            def group_exists(self, n=0):
                return not self.fixed or 0 <= self.it * (UNROLL // G) + self.k // G + n < NG

            def transfers(self, n=0):
                return self.it * 16 + 16 * ((self.k // G + n) // 2 + 1)

        def wait(eng, s, count):
            if not isinstance(count, int) or count > 0:
                eng.wait_ge(s, count)

        def run_steps(eng, step, first, last):
            for k in range(first, UNROLL):
                step(At(0, k))
            with eng.Fori(1, ITERS - 1) as it:
                for k in range(UNROLL):
                    step(At(it, k))
            for k in range(last + 1 - UNROLL * (ITERS - 1)):
                step(At(ITERS - 1, k))

        G_COUNTED, G_COPIED, G_VAR, G_DVE = 22, 26, 37, 43

        block = ctx.enter_context(nc.Block())

        @block.sync
        def _(sp):
            sp.dma_start(tab[:, :], table).then_inc(table_in, 16)
            sp.dma_start(x_in[0][:, 0:1, :], x_groups[0][:, 0:1, :]).then_inc(first_x_loaded, 16)
            sp.dma_start(adj_in[0][:, :, :], adj_groups[0]).then_inc(adj_loaded[0], 16)
            sp.dma_start(x_in[0][:, 1:G, :], x_groups[0][:, 1:G, :]).then_inc(x_loaded[0], 16)
            sp.dma_start(rel[:, :], rel_weights).then_inc(rel_in, 16)
            sp.dma_start(biases[:, :], bias_rows).then_inc(rel_in, 16)
            sp.dma_start(adj_in[1][:, :, :], adj_groups[1]).then_inc(adj_loaded[1], 16)
            sp.dma_start(x_in[1][:, :, :], x_groups[1]).then_inc(x_loaded[1], 16)

            def step(at):
                if at.j:
                    return
                s = at.gslot
                loads, stores = at.group_exists(2), at.group_exists(-1)
                to_load = at.group(1) if at.fixed else sp.snap(at.group(1))
                to_store = at.group(-2) if at.fixed else sp.snap(at.group(-2))
                if loads:
                    wait(sp, cast_done, at.group())
                    wait(sp, deg_done, at.group())
                    sp.dma_start(adj_in[s][:, :, :], dram(adj_groups, to_load)).then_inc(adj_loaded[s], 16)
                    wait(sp, resid_done, at.graphs(G - 1))
                    sp.dma_start(x_in[s][:, :, :], dram(x_groups, to_load)).then_inc(x_loaded[s], 16)
                if stores:
                    wait(sp, y_done, at.graphs(-1))
                    sp.dma_start(dram(out_groups, to_store), y_out[1 - s][:, :, :]).then_inc(stored[1 - s], 16)

            def dram(t, i):
                return t[i] if isinstance(i, int) else t[bass.ds(i, 1)].squeeze(0)

            run_steps(sp, step, 0, B - 1)
            for j in range(G):
                b = B - G + j
                sp.wait_ge(y_done, b + 1)
                sp.dma_start(out[b], y_out[(NG - 1) % 2][:, j, :]).then_inc(last_stored, 16)
            sp.wait_ge(flag_ready, 1)
            general_needed = sp.value_load(flag[0:1, 0:1], min_val=0, max_val=P) > 0
            for s in range(2):
                sp.wait_ge(stored[s], 16 * len(range(s, NG - 1, 2)))
            sp.wait_ge(last_stored, 16 * G)
            with sp.If(general_needed):
                sp.dma_start(g_iota[:, :], count_to_80).then_inc(g_moved, 16)
                for dst, row in ((ew_r[NUM_REL:NUM_REL + 1, :], B_R), (ew_rr[NUM_REL:NUM_REL + 1, :], B_RR),
                                 (g_bias[:, 0, :], B_ADJ), (g_bias[:, 1, :], B_REV), (g_bias[:, 2, :], B_SELF)):
                    sp.dma_start(dst, bias_rows[row:row + 1, :]).then_inc(g_moved, 16)
                with sp.Fori(0, B) as b:
                    sp.wait_ge(g_moved, b * 16 + 16 * 6)
                    sp.dma_start(gx[:, :], x[bass.ds(b, 1)].squeeze(0)).then_inc(g_loaded, 16)
                    sp.dma_start(gadj[:, :], adj[bass.ds(b, 1)].squeeze(0)).then_inc(g_loaded, 16)
                    sp.wait_ge(g_dve, (b + 1) * G_DVE)
                    sp.dma_start(out[bass.ds(b, 1)].squeeze(0), g_y[:, :]).then_inc(g_moved, 16)
                sp.wait_ge(g_moved, B * 16 + 16 * 6)
        @block.tensor
        def _(pe):
            def products(bank, slot, w_hi, w_lo, before, closed):
                terms = [(x_hi, w_hi), (x_hi, w_lo), (x_lo, w_hi)]
                for n, (lhs, rhs) in enumerate(terms):
                    for c in range(HC):
                        before(n, c)
                        last = nc.tensor.matmul(bank[:, 0:H], lhs[slot][:, c * N:(c + 1) * N], rhs[:, c, :],
                                                start=(n == 0 and c == 0),
                                                stop=(closed and n == len(terms) - 1 and c == HC - 1))
                return last

            def degree_rows(of):
                wait(pe, cast_done, of.group())
                wait(pe, odd_done, of.group(-1))
                nc.tensor.matmul(ps_chk[:, :], ones_r[:, :], a_r[of.gslot][:, :, :],
                                 start=True, stop=True).then_inc(deg_row_done, 1)

            def bias_product(of):
                if of.j == 0:
                    wait(pe, factors_done, of.group())
                nc.tensor.matmul(ps_s[of.slot][:, 0:H], factors[of.gslot][:, of.j, :], bias_rhs[:, :],
                                 start=False, stop=True).then_inc(s_done, 1)

            def transposed_group(of):
                for j in range(G):
                    last = nc.tensor.matmul(ps_chk[:, j * N:(j + 1) * N], a_r[of.gslot][:, j, :], ident_r[:, :],
                                            start=True, stop=True)
                last.then_inc(at_done, 1)

            def step(at):
                if at.exists():
                    wait(pe, x_hi_done, at.graphs())
                    wait(pe, z_lo_done, at.graphs(-2))

                    def before(term, c):
                        if at.is_graph(0) and term == 0:
                            wait(pe, nb_hi_done, c + 1)
                        if at.is_graph(0) and term == 1:
                            wait(pe, nb_lo_done, c + 1)
                        if term == 2 and c == 0:
                            wait(pe, x_lo_done, at.graphs())

                    products(ps_z[at.slot], at.slot, nb_hi, nb_lo, before, True).then_inc(z_done, 1)
                if at.is_graph(1):
                    wait(pe, bias_ready, 2)
                    bias_product(at + -1)
                    transposed_group(at + -1)
                nxt = at + 1
                if nxt.exists():
                    if nxt.is_graph(0):
                        wait(pe, table_in, 16)
                        wait(pe, first_x_loaded, 16)
                    elif nxt.j == 0 or nxt.is_graph(1):
                        wait(pe, x_loaded[nxt.gslot], nxt.transfers())
                    wait(pe, x_lo_done, nxt.graphs(-1))
                    for c in range(HC):
                        last = nc.tensor.transpose(ps_xt[:, c * N:(c + 1) * N],
                                                   x_in[nxt.gslot][:, nxt.j, c * P:(c + 1) * P], ident)
                    last.then_inc(xt_done, 1)
                prev = at + -1
                if prev.exists():
                    wait(pe, z_hi_done, prev.graphs())
                    wait(pe, ctx_done, prev.graphs(-2))
                    a = a_r[prev.gslot][:, prev.j, :]
                    nc.tensor.matmul(ps_c[prev.slot][:, 0:H], a, z_hi[prev.slot][:, :], start=True, stop=False)
                    wait(pe, z_lo_done, prev.graphs())
                    nc.tensor.matmul(ps_c[prev.slot][:, 0:H], a, z_lo[prev.slot][:, :],
                                     start=False, stop=True).then_inc(c_done, 1)
                if at.j == 2 and at.group_exists(1) and not at.is_graph(-2):
                    degree_rows(at + G)
                if at.exists():
                    wait(pe, t_done, at.graphs(-2))

                    def before(term, c):
                        if at.is_graph(0) and term == 0:
                            wait(pe, self_hi_done, c + 1)
                        if at.is_graph(0) and term == 1:
                            wait(pe, self_lo_done, c + 1)

                    bank = ps_s[at.slot]
                    products(bank, at.slot, self_hi, self_lo, before, False)
                    if at.is_graph(0):
                        pe.wait_ge(e_sel_ready, 2)
                        pe.wait_ge(rel_in, 32)
                        bias_bank = ps_s[1][0:KB, 0:H]
                        nc.tensor.matmul(bias_bank, e_sel[:, 0, :], rel[:, R_WR:R_WR + H], start=True, stop=False)
                        nc.tensor.matmul(bias_bank, e_sel[:, 1, :], rel[:, R_WRR:R_WRR + H], start=False, stop=False)
                        nc.tensor.matmul(bias_bank, tab[0:5, C_SEL:C_SEL + KB], biases[:, :],
                                         start=False, stop=True).then_inc(bias_summed, 1)
                        degree_rows(at)
                    if not at.is_graph(0):
                        bias_product(at)
                        if at.j == 0:
                            transposed_group(at)

            pe.wait_ge(consts_ready, 2)
            run_steps(pe, step, -2, B)

            pe.wait_ge(verdict_ready, 1)
            nc.tensor.matmul(ps_chk[0:1, 0:1], verdict[:, 0:1], ones[:, 0:1],
                             start=True, stop=True).then_inc(verdict_summed, 1)
            pe.wait_ge(flag_ready, 1)
            with pe.If(pe.value_load(flag[0:1, 0:1], min_val=0, max_val=P) > 0):
                for s, w in enumerate((R_WR, R_WRR)):
                    nc.tensor.matmul(banks[2 + s][0:NUM_REL, 0:H], rel[:, R_E:R_E + NUM_REL], rel[:, w:w + H],
                                     start=True, stop=True).then_inc(g_setup_pe, 1)
                pe.wait_ge(g_setup_dve, 2)
                with pe.Fori(0, B) as b:
                    pe.wait_ge(g_loaded, (b + 1) * 32)
                    pe.wait_ge(g_dve, b * G_DVE + 1)
                    for c in range(HC):
                        nc.tensor.transpose(banks[0][:, c * N:(c + 1) * N], gx[:, c * P:(c + 1) * P], ident)
                    nc.tensor.transpose(banks[1][:, 0:N], g_a[:, :], ident).then_inc(g_pe, 1)
                    pe.wait_ge(g_dve, b * G_DVE + G_COUNTED)
                    for s in range(2):
                        nc.tensor.transpose(banks[2 + s][0:NUM_REL + 1, 0:N], g_cnt[s][:, :], ident)
                    for s, w in enumerate((w_adj, w_rev)):
                        for c in range(HC):
                            nc.tensor.matmul(banks[4 + s][:, 0:H], g_xt[:, c * N:(c + 1) * N], w[:, c, :],
                                             start=(c == 0), stop=False)
                        last = nc.tensor.matmul(banks[4 + s][:, 0:H], ones[0:1, :], g_bias[:, s, :],
                                                start=False, stop=True)
                    last.then_inc(g_pe, 1)
                    pe.wait_ge(g_dve, b * G_DVE + G_COPIED)
                    nc.tensor.matmul(banks[6][:, 0:H], g_at[:, :], g_z[0][:, :], start=True, stop=True)
                    nc.tensor.matmul(banks[7][:, 0:H], g_a[:, :], g_z[1][:, :], start=True, stop=True)
                    for c in range(HC):
                        nc.tensor.matmul(banks[0][:, 0:H], g_xt[:, c * N:(c + 1) * N], w_self[:, c, :],
                                         start=(c == 0), stop=False)
                    nc.tensor.matmul(banks[0][:, 0:H], ones[0:1, :], g_bias[:, 2, :],
                                     start=False, stop=False)
                    nc.tensor.matmul(banks[0][:, 0:H], g_cnt_t[0][:, :], ew_r[:, :], start=False, stop=False)
                    nc.tensor.matmul(banks[0][:, 0:H], g_cnt_t[1][:, :], ew_rr[:, :],
                                     start=False, stop=True).then_inc(g_pe, 1)

        @block.scalar
        def _(act):
            by_chunk = "(c p) o -> p c o"
            act.dma_start(w_adj[:, :, :], WadjT.rearrange(by_chunk, p=P)).then_inc(nb_w_in, 16)
            act.dma_start(w_rev[:, :, :], WrevT.rearrange(by_chunk, p=P)).then_inc(nb_w_in, 16)
            act.dma_start(w_self[:, :, :], WselfT.rearrange(by_chunk, p=P)).then_inc(self_w_in, 16)

            def high_parts():
                for c in range(HC):
                    act.wait_ge(nb_sum_done, c + 1)
                    nc.scalar.copy(nb_hi[:, c, :], w_nb[:, c, :]).then_inc(nb_hi_done, 1)
                act.wait_ge(self_w_in, 16)
                for c in range(HC):
                    nc.scalar.copy(self_hi[:, c, :], w_self[:, c, :]).then_inc(self_hi_done, 1)

            def step(at):
                done = at + -NORM_LAG
                if done.exists():
                    if done.j == 0:
                        wait(act, rstd_done, done.group())
                        wait(act, shift_done, done.group())
                        wait(act, stored[done.gslot], done.transfers(-2))
                    nc.scalar.activation(y_out[done.gslot][:, done.j, :], t_sum[done.gslot][:, done.j, :],
                                         ACT.Identity, bias=shift[done.gslot][:, done.j:done.j + 1],
                                         scale=rstd[done.gslot][:, done.j:done.j + 1]).then_inc(y_done, 1)
                if at.j == 2 and at.group_exists(-1):
                    s = 1 - at.gslot
                    wait(act, var_eps_done, at.group(-1))
                    nc.scalar.activation(root[s][:, :], var_eps[s][:, :], ACT.Sqrt).then_inc(root_done, 1)
                if at.exists():
                    wait(act, z_done, at.graphs())
                    wait(act, c_done, at.graphs(-2))
                    nc.scalar.copy(z_hi[at.slot][:, :], ps_z[at.slot][:, 0:H]).then_inc(z_hi_done, 1)
                nxt = at + 1
                if nxt.exists():
                    wait(act, xt_done, nxt.graphs())
                    wait(act, s_done, nxt.graphs(-2))
                    nc.scalar.copy(x_hi[nxt.slot][:, :], ps_xt[:, 0:HC * N]).then_inc(x_hi_done, 1)
                if at.is_graph(-1):
                    high_parts()
                if at.is_graph(0):
                    act.wait_ge(bias_summed, 1)
                    nc.scalar.copy(bias_all[:, :], ps_s[1][0:KB, 0:H]).then_inc(bias_hi_done, 1)
                prev = at + -1
                if prev.exists():
                    wait(act, c_done, prev.graphs())
                    if prev.j == 0:
                        wait(act, inv_deg_done, prev.group())
                    wait(act, resid_done, prev.graphs(-2))
                    nc.scalar.activation(ctx_sb[prev.slot][:, :], ps_c[prev.slot][:, 0:H], ACT.Copy,
                                         scale=inv_deg[prev.gslot][:, prev.j:prev.j + 1]).then_inc(ctx_done, 1)

            run_steps(act, step, -1, B - 1 + NORM_LAG)
            act.wait_ge(flag_ready, 1)
            with act.If(act.value_load(flag[0:1, 0:1], min_val=0, max_val=P) > 0):
                with act.Fori(0, B) as b:
                    act.wait_ge(g_dve, b * G_DVE + G_VAR)
                    nc.scalar.activation(g_ln[:, 1:2], g_ln[:, 0:1], ACT.Sqrt).then_inc(g_act, 1)

        @block.gpsimd
        def _(pool):
            def step(at):
                cast = at.j == 0 and at.group_exists(1)
                s, nxt, prev = 1 - at.gslot, at + G, at + -1
                if cast:
                    wait(pool, adj_loaded[s], nxt.transfers())
                    wait(pool, c_done, at.graphs(-1))
                    wait(pool, odd_done, at.group(-1))
                if prev.exists():
                    wait(pool, t_done, prev.graphs(-2))
                    wait(pool, ctx_done, prev.graphs())
                    nc.gpsimd.tensor_tensor(resid[prev.slot][:, :], ctx_sb[prev.slot][:, :],
                                            x_in[prev.gslot][:, prev.j, :], ALU.add).then_inc(resid_done, 1)
                if cast:
                    nc.gpsimd.tensor_copy(a_r[s][:, :, :], adj_in[s][:, :, :]).then_inc(cast_done, 1)

            run_steps(pool, step, -4, B)

        def general(dve, b):
            n = [0]

            def link(ins):
                ins.then_inc(g_dve, 1)
                n[0] += 1
                dve.wait_ge(g_dve, b * G_DVE + n[0])

            def v(*a, **k):
                link(nc.vector.tensor_scalar(*a, **k))

            dve.wait_ge(g_loaded, (b + 1) * 32)
            link(nc.vector.tensor_copy(g_a[:, :], gadj[:, :]))
            dve.wait_ge(g_pe, b * 3 + 1)
            link(nc.vector.tensor_copy(g_xt[:, :], banks[0][:, 0:HC * N]))
            link(nc.vector.tensor_copy(g_at[:, :], banks[1][:, 0:N]))
            v(g_tmp[:, :], g_a[:, :], 0.0, float(NUM_REL), ALU.is_lt, ALU.mult)
            link(nc.vector.tensor_tensor(g_tmp[:, :], g_tmp[:, :], g_a[:, :], ALU.add))
            v(g_idx[:, 0, :], g_tmp[:, :], 0.0, float(NUM_REL - 1), ALU.max, ALU.min)
            v(g_tmp[:, :], g_at[:, :], float(NUM_BASE), float(NUM_REL - 1), ALU.add, ALU.min)
            v(g_idx[:, 1, :], g_at[:, :], 0.0, None, ALU.is_gt)
            link(nc.vector.tensor_tensor(g_idx[:, 1, :], g_idx[:, 1, :], g_tmp[:, :], ALU.mult))
            for s, a in enumerate((g_a, g_at)):
                def over_c(t):
                    return t.unsqueeze(1).to_broadcast([P, NUM_REL, N])
                iota = g_iota[:, :].unsqueeze(2).to_broadcast([P, NUM_REL, N])
                link(nc.vector.tensor_tensor(g_hot[:, :, :], over_c(g_idx[:, s, :]), iota, ALU.is_equal))
                link(nc.vector.tensor_tensor(g_hot[:, :, :], g_hot[:, :, :], over_c(a[:, :]), ALU.mult))
                link(nc.vector.tensor_reduce(g_cnt[s][:, 0:NUM_REL], g_hot[:, :, :], AX.X, ALU.add))
                link(nc.vector.tensor_reduce(g_cnt[s][:, NUM_REL:NUM_REL + 1], a[:, :], AX.X, ALU.add))
                d = g_cnt[s][:, NUM_REL:NUM_REL + 1]
                v(g_inv[:, s:s + 1], d, 0.0, None, ALU.is_le)
                link(nc.vector.scalar_tensor_tensor(out=g_inv[:, 2 + s:3 + s], in0=d, scalar=0.0,
                                                    in1=g_inv[:, s:s + 1], op0=ALU.max, op1=ALU.add))
            link(nc.vector.reciprocal(g_inv[:, 0:2], g_inv[:, 2:4]))
            assert n[0] == G_COUNTED
            dve.wait_ge(g_pe, b * 3 + 2)
            for s in range(2):
                link(nc.vector.tensor_copy(g_cnt_t[s][:, :], banks[2 + s][0:NUM_REL + 1, 0:N]))
                link(nc.vector.tensor_copy(g_z[s][:, :], banks[4 + s][:, 0:H]))
            assert n[0] == G_COPIED
            dve.wait_ge(g_pe, b * 3 + 3)
            for s, more in enumerate((gx, g_t)):
                link(nc.vector.scalar_tensor_tensor(out=g_t[:, :], in0=banks[6 + s][:, 0:H],
                                                    scalar=g_inv[:, s:s + 1], in1=more[:, :],
                                                    op0=ALU.mult, op1=ALU.add))
            link(nc.vector.tensor_tensor(g_t[:, :], banks[0][:, 0:H], g_t[:, :], ALU.add))
            link(nc.vector.bn_stats(g_stats[:, :], g_t[:, :]))
            st, m = g_stats, g_mv
            link(nc.vector.tensor_tensor(m[:, 0:1], st[:, 1:2], st[:, 4:5], ALU.add))
            v(m[:, 0:1], m[:, 0:1], 0.5, None, ALU.mult)
            link(nc.vector.tensor_tensor(m[:, 1:2], st[:, 1:2], st[:, 4:5], ALU.subtract))
            link(nc.vector.tensor_tensor(m[:, 2:3], m[:, 1:2], m[:, 1:2], ALU.mult))
            link(nc.vector.tensor_tensor(m[:, 3:4], st[:, 2:3], st[:, 5:6], ALU.add))
            v(m[:, 4:5], m[:, 3:4], 1.0 / H, EPS, ALU.mult, ALU.add)
            link(nc.vector.scalar_tensor_tensor(out=g_ln[:, 0:1], in0=m[:, 2:3], scalar=0.25, in1=m[:, 4:5],
                                                op0=ALU.mult, op1=ALU.add))
            assert n[0] == G_VAR
            dve.wait_ge(g_act, b + 1)
            link(nc.vector.reciprocal(g_ln[:, 2:3], g_ln[:, 1:2]))
            link(nc.vector.tensor_tensor(g_ln[:, 3:4], g_ln[:, 2:3], g_ln[:, 2:3], ALU.mult))
            link(nc.vector.tensor_tensor(g_ln[:, 4:5], g_ln[:, 3:4], g_ln[:, 0:1], ALU.mult))
            v(g_ln[:, 5:6], g_ln[:, 4:5], -0.5, 1.5, ALU.mult, ALU.add)
            link(nc.vector.tensor_tensor(g_ln[:, 6:7], g_ln[:, 5:6], g_ln[:, 2:3], ALU.mult))
            v(g_y[:, :], g_t[:, :], g_mv[:, 0:1], g_ln[:, 6:7], ALU.subtract, ALU.mult)
            assert n[0] == G_DVE

        @block.vector
        def _(dve):
            nc.vector.memset(odd_sum[:, :], 0.0).then_inc(odd_cleared, 1)
            nc.vector.memset(ones[:, :], 1.0).then_inc(odd_cleared, 1)
            nc.vector.memset(e_sel[:, :, :], 0.0).then_inc(e_sel_zero, 1)
            dve.wait_ge(odd_cleared, 2)
            nc.vector.tensor_copy(ones_r[:, :], ones[:, :]).then_inc(consts_ready, 1)
            dve.wait_ge(table_in, 16)
            nc.vector.tensor_copy(ident_r[:, :], ident).then_inc(consts_ready, 1)

            def weights():
                dve.wait_ge(nb_w_in, 32)
                for c in range(HC):
                    nc.vector.tensor_tensor(w_nb[:, c, :], w_adj[:, c, :], w_rev[:, c, :],
                                            ALU.add).then_inc(nb_sum_done, 1)
                for c in range(HC):
                    dve.wait_ge(nb_hi_done, c + 1)
                    nc.vector.tensor_tensor(nb_lo[:, c, :], w_nb[:, c, :], nb_hi[:, c, :].bitcast(fp32),
                                            ALU.subtract).then_inc(nb_lo_done, 1)
                for c in range(HC):
                    dve.wait_ge(self_hi_done, c + 1)
                    nc.vector.tensor_tensor(self_lo[:, c, :], w_self[:, c, :], self_hi[:, c, :].bitcast(fp32),
                                            ALU.subtract).then_inc(self_lo_done, 1)

            def bias_side():
                dve.wait_ge(rel_in, 32)
                dve.wait_ge(e_sel_zero, 1)
                for s, row in enumerate((1, NUM_BASE + 1)):
                    nc.vector.tensor_copy(e_sel[:, s, 0:LOW + 1:LOW],
                                          rel[:, R_E + row:R_E + row + 1].to_broadcast([R, 2])).then_inc(e_sel_ready, 1)
                dve.wait_ge(bias_hi_done, 1)
                nc.vector.tensor_copy(bias_rhs[0:LOW, :], bias_all[0:LOW, :].bitcast(fp32)).then_inc(bias_ready, 1)
                nc.vector.tensor_tensor(bias_rhs[LOW:KB, :], ps_s[1][LOW:KB, 0:H], bias_all[LOW:KB, :].bitcast(fp32),
                                        ALU.subtract).then_inc(bias_ready, 1)

            def degrees(of):
                s = of.gslot
                wait(dve, adj_loaded[s], of.transfers())
                nc.vector.tensor_reduce(deg[s][:, :], adj_in[s][:, :, :], AX.X, ALU.add).then_inc(deg_done, 1)
                wait(dve, deg_row_done, of.group())
                wait(dve, s_done, of.graphs(-1 - G - of.j))
                nc.vector.tensor_scalar(factors[s][:, :, :], ps_chk[0:KB, :].rearrange("p (j n) -> p j n", j=G),
                                        tab[0:KB, C_LIM:C_LIM + 1], tab[0:KB, C_LIM + 1:C_LIM + 2],
                                        ALU.max, ALU.min).then_inc(factors_done, 1)
                wait(dve, deg_done, of.group())
                nc.vector.tensor_scalar(deg[s][:, :], deg[s][:, :], 1.0, None, ALU.max).then_inc(deg_max_done, 1)
                wait(dve, deg_max_done, of.group())
                wait(dve, ctx_done, of.graphs(-1 - G - of.j))
                nc.vector.reciprocal(inv_deg[s][:, :], deg[s][:, :]).then_inc(inv_deg_done, 1)

            def step(at):
                old = at + -2
                if old.exists():
                    s = old.gslot
                    wait(dve, resid_done, old.graphs())
                    wait(dve, s_done, old.graphs())
                    wait(dve, y_done, old.graphs(-UNROLL - min(old.k, 0)))
                    nc.vector.tensor_tensor(t_sum[s][:, old.j, :], ps_s[old.slot][:, 0:H], resid[old.slot][:, :],
                                            ALU.add).then_inc(t_done, 1)
                if at.exists():
                    wait(dve, z_hi_done, at.graphs())
                    nc.vector.tensor_tensor(z_lo[at.slot][:, :], ps_z[at.slot][:, 0:H],
                                            z_hi[at.slot][:, :].bitcast(fp32), ALU.subtract).then_inc(z_lo_done, 1)
                nxt = at + 1
                if nxt.exists():
                    wait(dve, x_hi_done, nxt.graphs())
                    wait(dve, s_done, nxt.graphs(-2))
                    nc.vector.tensor_tensor(x_lo[nxt.slot][:, :], ps_xt[:, 0:HC * N],
                                            x_hi[nxt.slot][:, :].bitcast(fp32), ALU.subtract).then_inc(x_lo_done, 1)
                if old.exists():
                    wait(dve, t_done, old.graphs())
                    nc.vector.bn_stats(stats[old.gslot][:, old.j, :],
                                       t_sum[old.gslot][:, old.j, :]).then_inc(stats_done, 1)
                if at.j == 1 and at.group_exists(-1):
                    s = 1 - at.gslot
                    wait(dve, stats_done, at.graphs(-2))
                    m, st, steps = moments[s], stats[s], 5 * at.group(-1)
                    nc.vector.tensor_tensor(m[:, 0, :], st[:, :, 1], st[:, :, 4], ALU.add).then_inc(moments_done, 1)
                    nc.vector.tensor_tensor(m[:, 1, :], st[:, :, 1], st[:, :, 4], ALU.subtract).then_inc(moments_done, 1)
                    nc.vector.tensor_tensor(m[:, 2, :], st[:, :, 2], st[:, :, 5], ALU.add).then_inc(moments_done, 1)
                    wait(dve, moments_done, steps - 3)
                    nc.vector.tensor_tensor(m[:, 3, :], m[:, 1, :], m[:, 1, :], ALU.mult).then_inc(moments_done, 1)
                    wait(dve, moments_done, steps - 2)
                    nc.vector.tensor_scalar(m[:, 4, :], m[:, 2, :], 1.0 / H, EPS, ALU.mult, ALU.add).then_inc(moments_done, 1)
                    wait(dve, moments_done, steps)
                    nc.vector.scalar_tensor_tensor(out=var_eps[s][:, :], in0=m[:, 3, :], scalar=0.25, in1=m[:, 4, :],
                                                   op0=ALU.mult, op1=ALU.add).then_inc(var_eps_done, 1)
                if at.j == 1 and at.group_exists():
                    s = at.gslot
                    wait(dve, at_done, at.group())
                    nc.vector.scalar_tensor_tensor(out=odd_scratch[:, :, :],
                                                   in0=ps_chk[:, :].rearrange("p (j n) -> p j n", j=G), scalar=0.0,
                                                   in1=a_r[s][:, :, :].bitcast(fp32), op0=ALU.is_gt,
                                                   op1=ALU.not_equal, accum_out=odd[:, s:s + 1]).then_inc(odd_done, 1)
                    wait(dve, odd_done, at.group())
                    wait(dve, odd_summed, at.group(-1))
                    wait(dve, odd_cleared, 2)
                    nc.vector.tensor_tensor(odd_sum[:, :], odd_sum[:, :], odd[:, s:s + 1],
                                            ALU.add).then_inc(odd_summed, 1)
                if at.j == 2 and at.group_exists(-1):
                    s = 1 - at.gslot
                    w, steps = newton[s], 4 * at.group(-1)
                    wait(dve, root_done, at.group(-1))
                    nc.vector.reciprocal(w[:, 0, :], root[s][:, :]).then_inc(newton_done, 1)
                    wait(dve, newton_done, steps - 3)
                    nc.vector.tensor_tensor(w[:, 1, :], w[:, 0, :], w[:, 0, :], ALU.mult).then_inc(newton_done, 1)
                    wait(dve, newton_done, steps - 2)
                    nc.vector.tensor_tensor(w[:, 2, :], w[:, 1, :], var_eps[s][:, :], ALU.mult).then_inc(newton_done, 1)
                    wait(dve, newton_done, steps - 1)
                    nc.vector.tensor_scalar(w[:, 3, :], w[:, 2, :], -0.5, 1.5, ALU.mult, ALU.add).then_inc(newton_done, 1)
                    wait(dve, newton_done, steps)
                    nc.vector.tensor_tensor(rstd[s][:, :], w[:, 3, :], w[:, 0, :], ALU.mult).then_inc(rstd_done, 1)
                    wait(dve, rstd_done, at.group(-1))
                    nc.vector.scalar_tensor_tensor(out=shift[s][:, :], in0=moments[s][:, 0, :], scalar=-0.5,
                                                   in1=rstd[s][:, :], op0=ALU.mult, op1=ALU.mult).then_inc(shift_done, 1)
                if at.is_graph(-1):
                    weights()
                if at.is_graph(0):
                    bias_side()
                    degrees(at)
                if at.j == 3 and at.group_exists(1) and not at.is_graph(-1):
                    degrees(at + 1)
                if at.is_graph(B - G + 1):
                    dve.wait_ge(odd_summed, NG)
                    nc.vector.tensor_scalar(verdict[:, :], odd_sum[:, :], 0.0, None, ALU.is_gt).then_inc(verdict_ready, 1)

            run_steps(dve, step, -2, B + 2)

            dve.wait_ge(verdict_summed, 1)
            nc.vector.tensor_copy(flag[:, :], ps_chk[0:1, 0:1]).then_inc(flag_ready, 1)
            dve.wait_ge(flag_ready, 1)
            with dve.If(dve.value_load(flag[0:1, 0:1], min_val=0, max_val=P) > 0):
                for s, t in enumerate((ew_r, ew_rr)):
                    dve.wait_ge(g_setup_pe, s + 1)
                    nc.vector.tensor_copy(t[0:NUM_REL, :], banks[2 + s][0:NUM_REL, 0:H]).then_inc(g_setup_dve, 1)
                dve.wait_ge(g_moved, 16 * 6)
                with dve.Fori(0, B) as b:
                    general(dve, b)


def kernel(x, adj, L0_gnn_E, L0_gnn_Wadj, L0_gnn_badj, L0_gnn_Wrev, L0_gnn_brev, L0_gnn_Wself, L0_gnn_bself,
           L0_gnn_Wr, L0_gnn_br, L0_gnn_Wrr, L0_gnn_brr):
    import numpy as np
    import concourse.bacc as bacc
    from concourse.bass_utils import run_bass_kernel_spmd

    arrays = {"x": x, "adj": adj}
    for name, a in (("WadjT", L0_gnn_Wadj), ("WrevT", L0_gnn_Wrev), ("WselfT", L0_gnn_Wself)):
        arrays[name] = np.asarray(a).T
    arrays["rel_weights"] = np.concatenate([np.asarray(a).T for a in (L0_gnn_E, L0_gnn_Wr, L0_gnn_Wrr)], axis=1)
    arrays["bias_rows"] = np.stack([np.asarray(a) for a in (L0_gnn_badj, L0_gnn_brev, L0_gnn_bself,
                                                            L0_gnn_br, L0_gnn_brr)])
    arrays["table"], arrays["count_to_80"] = constants()

    nc = bacc.Bacc("TRN2", target_bir_lowering=False, num_devices=1)
    arrays = {name: np.ascontiguousarray(a) for name, a in arrays.items()}
    tensors = {name: nc.dram_tensor(name, a.shape, mybir.dt.from_np(a.dtype), kind="ExternalInput").ap()
               for name, a in arrays.items()}
    out = nc.dram_tensor("out", (B, N, H), fp32, kind="ExternalOutput").ap()
    graph_layer(nc, out=out, **tensors)
    return run_bass_kernel_spmd(nc, [arrays], core_ids=[0]).results[0]["out"]
```

```python
from contextlib import ExitStack

import concourse.bass as bass
from concourse import mybir

fp32 = mybir.dt.float32
fp32r = mybir.dt.float32r
i32 = mybir.dt.int32
ALU = mybir.AluOpType
ACT = mybir.ActivationFunctionType
AX = mybir.AxisListType

B, N, H = 64, 128, 384
R = 128
NUM_REL, NUM_BASE = 80, 40
P = 128
HC = H // P
G = 4
NG = B // G
UNROLL = 2 * G
ITERS = B // UNROLL
EPS = 1e-5
NORM_LAG = 6
WARM = 10
KB = 64
LOW = 32

C_ID = 0
C_SEL = C_ID + P
C_LIM = C_SEL + KB
C_END = C_LIM + 2
R_E, R_WR, R_WRR, R_END = 0, NUM_REL, NUM_REL + H, NUM_REL + 2 * H
B_ADJ, B_REV, B_SELF, B_R, B_RR = range(5)


def constants():
    import numpy as np

    t = np.zeros((P, C_END), np.float32)
    t[:, C_ID:C_ID + P] = np.eye(P)
    for m in (0, LOW):
        t[[B_R, B_RR], C_SEL + m] = 1.0
        t[B_SELF, C_SEL + m + 1] = 1.0
        t[[B_ADJ, B_REV], C_SEL + m + 2] = 1.0
        t[m, C_LIM:C_LIM + 2] = 0.0, N
        t[m + 1, C_LIM:C_LIM + 2] = 1.0, 1.0
        t[m + 2, C_LIM:C_LIM + 2] = 0.0, 1.0
    return t, np.tile(np.arange(NUM_REL, dtype=np.float32), (P, 1))


def graph_layer(nc, x_t, adj, WadjT, WrevT, WselfT, rel_weights, bias_rows, table, count_to_80, out):
    x_groups = x_t.rearrange("(g e) p f -> g p e f", e=G)
    adj_groups = adj.rearrange("(g e) i j -> g i e j", e=G)
    out_groups = out.rearrange("(g e) i h -> g i e h", e=G)

    with ExitStack() as ctx:
        def sb(name, shape, dt=fp32):
            return ctx.enter_context(nc.sbuf_tensor(name, shape, dt))

        def sem(name):
            return ctx.enter_context(nc.semaphore(name))

        tab = sb("tab", [P, C_END])
        ident = tab[:, C_ID:C_ID + P]
        ones = sb("ones", [P, P])
        ones_r = sb("ones_r", [P, P], fp32r)
        w_adj = sb("w_adj", [P, HC, H])
        w_rev = sb("w_rev", [P, HC, H])
        w_self = sb("w_self", [P, HC, H])
        w_nb = sb("w_nb", [P, HC, H])
        nb_hi = sb("nb_hi", [P, HC, H], fp32r)
        nb_lo = sb("nb_lo", [P, HC, H], fp32r)
        self_hi = sb("self_hi", [P, HC, H], fp32r)
        self_lo = sb("self_lo", [P, HC, H], fp32r)
        rel = sb("rel", [R, R_END])
        e_sel = sb("e_sel", [R, 2, KB])
        biases = sb("biases", [5, H])
        bias_all = sb("bias_all", [KB, H], fp32r)
        bias_rhs = sb("bias_rhs", [KB, H], fp32r)

        x_in = [sb(f"x_in{s}", [P, G, HC * N]) for s in range(2)]
        adj_in = [sb(f"adj_in{s}", [P, G, N], i32) for s in range(2)]
        a_r = [sb(f"a_r{s}", [P, G, N], fp32r) for s in range(2)]
        t_sum = [sb(f"t_sum{s}", [P, G, H]) for s in range(2)]
        y_out = [sb(f"y_out{s}", [P, G, H]) for s in range(2)]
        factors = [sb(f"factors{s}", [KB, G, N], fp32r) for s in range(2)]
        deg = [sb(f"deg{s}", [P, G]) for s in range(2)]
        inv_deg = [sb(f"inv_deg{s}", [P, G]) for s in range(2)]
        stats = [sb(f"stats{s}", [P, G, 6]) for s in range(2)]
        moments = [sb(f"moments{s}", [P, 5, G]) for s in range(2)]
        var_eps = [sb(f"var_eps{s}", [P, G]) for s in range(2)]
        root = [sb(f"root{s}", [P, G]) for s in range(2)]
        newton = [sb(f"newton{s}", [P, 4, G]) for s in range(2)]
        rstd = [sb(f"rstd{s}", [P, G]) for s in range(2)]
        shift = [sb(f"shift{s}", [P, G]) for s in range(2)]
        odd_scratch = sb("odd_scratch", [P, N])
        x_hi = [sb(f"x_hi{s}", [P, HC * N], fp32r) for s in range(2)]
        x_lo = [sb(f"x_lo{s}", [P, HC * N], fp32r) for s in range(2)]
        z_hi = [sb(f"z_hi{s}", [P, H + P], fp32r) for s in range(2)]
        z_lo = [sb(f"z_lo{s}", [P, H], fp32r) for s in range(2)]
        s_sb = [sb(f"s_sb{s}", [P, H]) for s in range(2)]
        odd = sb("odd", [P, UNROLL])
        odd_sum = sb("odd_sum", [P, G])
        odd_total = sb("odd_total", [P, 1])
        verdict = sb("verdict", [P, 1])
        flag = sb("flag", [1, 1], i32)
        gadj = sb("gadj", [P, N], i32)
        g_a = sb("g_a", [P, N])
        g_at = sb("g_at", [P, N])
        g_xt = sb("g_xt", [P, HC * N])
        g_idx = sb("g_idx", [P, 2, N])
        g_tmp = sb("g_tmp", [P, N])
        g_hot = sb("g_hot", [P, NUM_REL, N])
        g_cnt = [sb(f"g_cnt{s}", [P, NUM_REL + 1]) for s in range(2)]
        g_cnt_t = [sb(f"g_cnt_t{s}", [NUM_REL + 1, N]) for s in range(2)]
        g_inv = sb("g_inv", [P, 4])
        g_z = [sb(f"g_z{s}", [P, H]) for s in range(2)]
        g_t = sb("g_t", [P, H])
        g_stats = sb("g_stats", [P, 6])
        g_mv = sb("g_mv", [P, 5])
        g_ln = sb("g_ln", [P, 8])
        g_y = sb("g_y", [P, H])
        g_bias = sb("g_bias", [1, 3, H])
        g_iota = sb("g_iota", [P, NUM_REL])
        ew_r = sb("ew_r", [NUM_REL + 1, H])
        ew_rr = sb("ew_rr", [NUM_REL + 1, H])

        banks = [ctx.enter_context(nc.psum_tensor(f"bank{i}", [P, 512], fp32)) for i in range(8)]
        ps_deg = banks[0]
        ps_z = banks[2:4]
        ps_s = banks[4:6]
        ps_c = banks[6:8]

        table_in = sem("table_in")
        nb_w_in = [sem(f"nb_w_in{c}") for c in range(HC)]
        self_w_in = [sem(f"self_w_in{c}") for c in range(HC)]
        rel_in = sem("rel_in")
        first_x_loaded = [sem(f"first_x_loaded{b}") for b in range(2)]
        x_loaded = [sem(f"x_loaded{s}") for s in range(2)]
        adj_loaded = [sem(f"adj_loaded{s}") for s in range(2)]
        stored = [sem(f"stored{s}") for s in range(2)]
        nb_sum_done = sem("nb_sum_done")
        nb_hi_done = sem("nb_hi_done")
        nb_lo_done = sem("nb_lo_done")
        identity_added = sem("identity_added")
        self_hi_done = sem("self_hi_done")
        self_lo_done = sem("self_lo_done")
        consts_ready = sem("consts_ready")
        e_sel_zero = sem("e_sel_zero")
        e_sel_ready = sem("e_sel_ready")
        bias_summed = sem("bias_summed")
        bias_hi_done = sem("bias_hi_done")
        bias_ready = sem("bias_ready")
        x_hi_done = sem("x_hi_done")
        x_lo_done = sem("x_lo_done")
        z_done = sem("z_done")
        z_hi_done = sem("z_hi_done")
        z_lo_done = sem("z_lo_done")
        c_done = sem("c_done")
        odd_done = sem("odd_done")
        s_done = sem("s_done")
        s_copied = sem("s_copied")
        t_done = sem("t_done")
        stats_done = sem("stats_done")
        y_done = sem("y_done")
        last_y_done = sem("last_y_done")
        cast_done = sem("cast_done")
        odd_summed = sem("odd_summed")
        deg_row_done = sem("deg_row_done")
        factors_done = sem("factors_done")
        deg_done = sem("deg_done")
        deg_max_done = sem("deg_max_done")
        inv_deg_done = sem("inv_deg_done")
        moments_done = sem("moments_done")
        var_eps_done = sem("var_eps_done")
        root_done = sem("root_done")
        newton_done = sem("newton_done")
        rstd_done = sem("rstd_done")
        shift_done = sem("shift_done")
        odd_cleared = sem("odd_cleared")
        odd_totalled = sem("odd_totalled")
        verdict_ready = sem("verdict_ready")
        verdict_summed = sem("verdict_summed")
        flag_ready = sem("flag_ready")
        g_moved = sem("g_moved")
        g_setup_pe = sem("g_setup_pe")
        g_setup_dve = sem("g_setup_dve")
        last_stored = sem("last_stored")
        g_loaded = sem("g_loaded")
        g_pe = sem("g_pe")
        g_dve = sem("g_dve")
        g_act = sem("g_act")

        class At:

            def __init__(self, it, k):
                self.it, self.k = it, k
                self.fixed = isinstance(it, int)
                self.slot, self.j, self.gslot = k % 2, k % G, (k // G) % 2

            def __add__(self, n):
                return At(self.it, self.k + n)

            def exists(self):
                return not self.fixed or 0 <= UNROLL * self.it + self.k < B

            def is_graph(self, b):
                return self.fixed and UNROLL * self.it + self.k == b

            def graphs(self, n=0):
                return self.it * UNROLL + (self.k + 1 + n)

            def group(self, n=0):
                return self.it * (UNROLL // G) + (self.k // G + 1 + n)

            def group_exists(self, n=0):
                return not self.fixed or 0 <= self.it * (UNROLL // G) + self.k // G + n < NG

            def transfers(self, n=0):
                return self.it * 16 + 16 * ((self.k // G + n) // 2 + 1)

        def x_parts_free(of):
            if of.is_graph(2) or of.is_graph(3):
                return z_done, of.graphs(-2)
            return s_done, of.graphs(-2)

        def wait(eng, s, count):
            if not isinstance(count, int) or count > 0:
                eng.wait_ge(s, count)

        def run_steps(eng, step, first, last):
            for k in range(first, UNROLL):
                step(At(0, k))
            with eng.Fori(1, ITERS - 1) as it:
                for k in range(UNROLL):
                    step(At(it, k))
            for k in range(last + 1 - UNROLL * (ITERS - 1)):
                step(At(ITERS - 1, k))

        LAST, EARLY, LATE = (NG - 1) % 2, slice(0, G // 2), slice(G // 2, G)
        G_COUNTED, G_COPIED, G_VAR, G_DVE = 21, 25, 36, 42

        block = ctx.enter_context(nc.Block())

        @block.sync
        def _(sp):
            sp.dma_start(tab[:, :], table).then_inc(table_in, 16)
            sp.dma_start(x_in[0][:, 0:1, :], x_groups[0][:, 0:1, :]).then_inc(first_x_loaded[0], 16)
            for c in range(HC):
                sp.dma_start(w_self[:, c, :], WselfT[c * P:(c + 1) * P, :]).then_inc(self_w_in[c], 16)
            sp.dma_start(x_in[0][:, 1:2, :], x_groups[0][:, 1:2, :]).then_inc(first_x_loaded[1], 16)
            for c in range(HC):
                rows = slice(c * P, (c + 1) * P)
                sp.dma_start(w_adj[:, c, :], WadjT[rows, :]).then_inc(nb_w_in[c], 16)
                sp.dma_start(w_rev[:, c, :], WrevT[rows, :]).then_inc(nb_w_in[c], 16)
            sp.dma_start(adj_in[0][:, :, :], adj_groups[0]).then_inc(adj_loaded[0], 16)
            sp.dma_start(x_in[0][:, 2:G, :], x_groups[0][:, 2:G, :]).then_inc(x_loaded[0], 16)
            sp.dma_start(rel[:, :], rel_weights).then_inc(rel_in, 16)
            sp.dma_start(biases[:, :], bias_rows).then_inc(rel_in, 16)
            sp.dma_start(adj_in[1][:, :, :], adj_groups[1]).then_inc(adj_loaded[1], 16)
            sp.dma_start(x_in[1][:, :, :], x_groups[1]).then_inc(x_loaded[1], 16)

            def step(at):
                if at.j:
                    return
                s = at.gslot
                loads, stores = at.group_exists(2), at.group_exists(-1)
                to_load = at.group(1) if at.fixed else sp.snap(at.group(1))
                to_store = at.group(-2) if at.fixed else sp.snap(at.group(-2))
                if loads:
                    wait(sp, cast_done, at.group())
                    wait(sp, deg_done, at.group())
                    sp.dma_start(adj_in[s][:, :, :], dram(adj_groups, to_load)).then_inc(adj_loaded[s], 16)
                    wait(sp, x_lo_done, at.graphs(G - 1))
                    sp.dma_start(x_in[s][:, :, :], dram(x_groups, to_load)).then_inc(x_loaded[s], 16)
                if stores:
                    wait(sp, y_done, at.graphs(-1))
                    sp.dma_start(dram(out_groups, to_store), y_out[1 - s][:, :, :]).then_inc(stored[1 - s], 16)

            def dram(t, i):
                return t[i] if isinstance(i, int) else t[bass.ds(i, 1)].squeeze(0)

            run_steps(sp, step, 0, B - 1)
            for e in range(G):
                if e < G - 1:
                    sp.wait_ge(y_done, B - G + e + 1)
                else:
                    sp.wait_ge(last_y_done, 1)
                sp.dma_start(out[B - G + e], y_out[LAST][:, e, :]).then_inc(last_stored, 16)
            sp.wait_ge(flag_ready, 1)
            general_needed = sp.value_load(flag[0:1, 0:1], min_val=0, max_val=P) > 0
            for s in range(2):
                sp.wait_ge(stored[s], 16 * len(range(s, NG - 1, 2)))
            sp.wait_ge(last_stored, 16 * G)
            with sp.If(general_needed):
                sp.dma_start(g_iota[:, :], count_to_80).then_inc(g_moved, 16)
                for dst, row in ((ew_r[NUM_REL:NUM_REL + 1, :], B_R), (ew_rr[NUM_REL:NUM_REL + 1, :], B_RR),
                                 (g_bias[:, 0, :], B_ADJ), (g_bias[:, 1, :], B_REV), (g_bias[:, 2, :], B_SELF)):
                    sp.dma_start(dst, bias_rows[row:row + 1, :]).then_inc(g_moved, 16)
                with sp.Fori(0, B) as b:
                    sp.wait_ge(g_moved, b * 16 + 16 * 6)
                    sp.dma_start(g_xt[:, :], x_t[bass.ds(b, 1)].squeeze(0)).then_inc(g_loaded, 16)
                    sp.dma_start(gadj[:, :], adj[bass.ds(b, 1)].squeeze(0)).then_inc(g_loaded, 16)
                    sp.wait_ge(g_dve, (b + 1) * G_DVE)
                    sp.dma_start(out[bass.ds(b, 1)].squeeze(0), g_y[:, :]).then_inc(g_moved, 16)
                sp.wait_ge(g_moved, B * 16 + 16 * 6)

        @block.tensor
        def _(pe):
            def warm_up(count):
                for i in range(count):
                    nc.tensor.matmul(ps_c[i % 2][:, :], ones_r[:, :],
                                     ones_r[:, :].unsqueeze(1).to_broadcast([P, G, P]), start=True, stop=True)

            def products(bank, slot, w_hi, w_lo, before, closed):
                terms = [(x_hi, w_hi), (x_lo, w_hi), (x_hi, w_lo)]
                for n, (lhs, rhs) in enumerate(terms):
                    for c in range(HC):
                        before(n, c)
                        last = nc.tensor.matmul(bank[:, 0:H], lhs[slot][:, c * N:(c + 1) * N], rhs[:, c, :],
                                                start=(n == 0 and c == 0),
                                                stop=(closed and n == len(terms) - 1 and c == HC - 1))
                return last

            def neighbour_product(of):
                wait(pe, z_hi_done, of.graphs())
                wait(pe, t_done, of.graphs(-2))
                wait(pe, odd_done, of.graphs(-2))
                if of.is_graph(0):
                    wait(pe, consts_ready, 3)
                a = a_r[of.gslot][:, of.j, :]
                nc.tensor.matmul(ps_c[of.slot][:, :], a, z_hi[of.slot][:, :], start=True, stop=False)
                wait(pe, z_lo_done, of.graphs())
                nc.tensor.matmul(ps_c[of.slot][:, 0:H], a, z_lo[of.slot][:, :],
                                 start=False, stop=True).then_inc(c_done, 1)

            def own_products(of):
                wait(pe, x_hi_done, of.graphs())
                wait(pe, s_copied, of.graphs(-2))

                def before(term, c):
                    if of.is_graph(0) and term == 0:
                        wait(pe, self_hi_done, c + 1)
                    if term == 1 and c == 0:
                        wait(pe, x_lo_done, of.graphs())
                    if of.is_graph(0) and term == 2:
                        wait(pe, self_lo_done, c + 1)

                products(ps_s[of.slot], of.slot, self_hi, self_lo, before, False)

            def degree_rows(of):
                wait(pe, cast_done, of.group())
                wait(pe, factors_done, of.group(-1))
                nc.tensor.matmul(ps_deg[:, :], ones_r[:, :], a_r[of.gslot][:, :, :],
                                 start=True, stop=True).then_inc(deg_row_done, 1)

            def bias_product(of):
                if of.j == 0:
                    wait(pe, factors_done, of.group())
                nc.tensor.matmul(ps_s[of.slot][:, 0:H], factors[of.gslot][:, of.j, :], bias_rhs[:, :],
                                 start=False, stop=True).then_inc(s_done, 1)

            def step(at):
                if at.is_graph(0):
                    own_products(at)
                    own_products(at + 1)
                wait(pe, x_hi_done, at.graphs())
                wait(pe, z_lo_done, at.graphs(-2))

                def before(term, c):
                    if at.is_graph(0) and term == 0:
                        wait(pe, nb_hi_done, c + 1)
                    if at.is_graph(0) and term == 2:
                        wait(pe, nb_lo_done, c + 1)
                    if term == 1 and c == 0:
                        wait(pe, x_lo_done, at.graphs())

                products(ps_z[at.slot], at.slot, nb_hi, nb_lo, before, True).then_inc(z_done, 1)
                if at.is_graph(2):
                    wait(pe, bias_ready, 2)
                    bias_product(at + -2)
                    bias_product(at + -1)
                if at.is_graph(1):
                    degree_rows(at + -1)
                if (at + -1).exists():
                    neighbour_product(at + -1)
                if at.is_graph(1):
                    pe.wait_ge(e_sel_ready, 2)
                    pe.wait_ge(rel_in, 32)
                    bias_bank = ps_c[1][0:KB, 0:H]
                    nc.tensor.matmul(bias_bank, e_sel[:, 0, :], rel[:, R_WR:R_WR + H], start=True, stop=False)
                    nc.tensor.matmul(bias_bank, e_sel[:, 1, :], rel[:, R_WRR:R_WRR + H], start=False, stop=False)
                    nc.tensor.matmul(bias_bank, tab[0:5, C_SEL:C_SEL + KB], biases[:, :],
                                     start=False, stop=True).then_inc(bias_summed, 1)
                if at.j == 3 and at.group_exists(1):
                    degree_rows(at + 1)
                if not at.is_graph(0) and not at.is_graph(1):
                    own_products(at)
                    bias_product(at)

            pe.wait_ge(consts_ready, 1)
            warm_up(WARM)
            run_steps(pe, step, 0, B - 1)
            neighbour_product(At(ITERS - 1, UNROLL - 1))

            pe.wait_ge(verdict_ready, 1)
            nc.tensor.matmul(ps_deg[0:1, 0:1], verdict[:, 0:1], ones[:, 0:1],
                             start=True, stop=True).then_inc(verdict_summed, 1)
            pe.wait_ge(flag_ready, 1)
            with pe.If(pe.value_load(flag[0:1, 0:1], min_val=0, max_val=P) > 0):
                for s, w in enumerate((R_WR, R_WRR)):
                    nc.tensor.matmul(banks[2 + s][0:NUM_REL, 0:H], rel[:, R_E:R_E + NUM_REL], rel[:, w:w + H],
                                     start=True, stop=True).then_inc(g_setup_pe, 1)
                pe.wait_ge(g_setup_dve, 2)
                with pe.Fori(0, B) as b:
                    pe.wait_ge(g_loaded, (b + 1) * 32)
                    pe.wait_ge(g_dve, b * G_DVE + 1)
                    nc.tensor.transpose(banks[1][:, 0:N], g_a[:, :], ident).then_inc(g_pe, 1)
                    pe.wait_ge(g_dve, b * G_DVE + G_COUNTED)
                    for s in range(2):
                        nc.tensor.transpose(banks[2 + s][0:NUM_REL + 1, 0:N], g_cnt[s][:, :], ident)
                    for s, w in enumerate((w_adj, w_rev)):
                        for c in range(HC):
                            nc.tensor.matmul(banks[4 + s][:, 0:H], g_xt[:, c * N:(c + 1) * N], w[:, c, :],
                                             start=(c == 0), stop=False)
                        last = nc.tensor.matmul(banks[4 + s][:, 0:H], ones[0:1, :], g_bias[:, s, :],
                                                start=False, stop=True)
                    last.then_inc(g_pe, 1)
                    pe.wait_ge(g_dve, b * G_DVE + G_COPIED)
                    nc.tensor.matmul(banks[6][:, 0:H], g_at[:, :], g_z[0][:, :], start=True, stop=True)
                    nc.tensor.matmul(banks[7][:, 0:H], g_a[:, :], g_z[1][:, :], start=True, stop=True)
                    for c in range(HC):
                        nc.tensor.matmul(banks[0][:, 0:H], g_xt[:, c * N:(c + 1) * N], w_self[:, c, :],
                                         start=(c == 0), stop=False)
                    nc.tensor.matmul(banks[0][:, 0:H], ones[0:1, :], g_bias[:, 2, :],
                                     start=False, stop=False)
                    nc.tensor.matmul(banks[0][:, 0:H], g_cnt_t[0][:, :], ew_r[:, :], start=False, stop=False)
                    nc.tensor.matmul(banks[0][:, 0:H], g_cnt_t[1][:, :], ew_rr[:, :],
                                     start=False, stop=True).then_inc(g_pe, 1)

        @block.scalar
        def _(act):
            def high_part_of_x(of):
                if of.is_graph(0) or of.is_graph(1):
                    wait(act, first_x_loaded[of.k], 16)
                elif of.j == 0 or of.is_graph(2):
                    wait(act, x_loaded[of.gslot], of.transfers())
                wait(act, *x_parts_free(of))
                nc.scalar.copy(x_hi[of.slot][:, :], x_in[of.gslot][:, of.j, :]).then_inc(x_hi_done, 1)

            def high_parts(nxt):
                for c in range(HC):
                    act.wait_ge(identity_added, c + 1)
                    nc.scalar.copy(self_hi[:, c, :], w_self[:, c, :]).then_inc(self_hi_done, 1)
                high_part_of_x(nxt)
                for c in range(HC):
                    act.wait_ge(nb_sum_done, c + 1)
                    nc.scalar.copy(nb_hi[:, c, :], w_nb[:, c, :]).then_inc(nb_hi_done, 1)

            def normalise(done):
                if done.j == 0:
                    wait(act, rstd_done, done.group())
                    wait(act, shift_done, done.group())
                    wait(act, stored[done.gslot], done.transfers(-2))
                nc.scalar.activation(y_out[done.gslot][:, done.j, :], t_sum[done.gslot][:, done.j, :],
                                     ACT.Identity, bias=shift[done.gslot][:, done.j:done.j + 1],
                                     scale=rstd[done.gslot][:, done.j:done.j + 1]).then_inc(y_done, 1)

            def square_root(s, part, count):
                wait(act, var_eps_done, count)
                nc.scalar.activation(root[s][:, part], var_eps[s][:, part], ACT.Sqrt).then_inc(root_done, 1)

            def cast(of):
                s = of.gslot
                wait(act, adj_loaded[s], of.transfers())
                wait(act, c_done, of.graphs(-1 - G - of.j))
                wait(act, odd_done, of.graphs(-1 - G - of.j))
                nc.scalar.copy(a_r[s][:, :, :], adj_in[s][:, :, :]).then_inc(cast_done, 1)

            def copy_s(of):
                wait(act, s_done, of.graphs())
                wait(act, t_done, of.graphs(-2))
                nc.scalar.copy(s_sb[of.slot][:, :], ps_s[of.slot][:, 0:H]).then_inc(s_copied, 1)

            def step(at):
                if (at + 1).exists() and not at.is_graph(0):
                    high_part_of_x(at + 1)
                if at.is_graph(-1):
                    high_parts(at + 2)
                if (at + -1).exists() and not at.is_graph(1):
                    copy_s(at + -1)
                done = at + -NORM_LAG
                if done.exists():
                    normalise(done)
                if at.j == 1 and at.group_exists(-1):
                    square_root(1 - at.gslot, slice(0, G), at.group(-1))
                if at.is_graph(B - 1):
                    square_root(LAST, EARLY, NG)
                if at.exists():
                    wait(act, z_done, at.graphs())
                    wait(act, c_done, at.graphs(-2))
                    nc.scalar.copy(z_hi[at.slot][:, 0:H], ps_z[at.slot][:, 0:H]).then_inc(z_hi_done, 1)
                if at.is_graph(0):
                    cast(at)
                if at.is_graph(1):
                    act.wait_ge(bias_summed, 1)
                    nc.scalar.copy(bias_all[:, :], ps_c[1][0:KB, 0:H]).then_inc(bias_hi_done, 1)
                if at.j == 1 and at.group_exists(1) and at.exists():
                    cast(at + (G - 1))
                if at.is_graph(1):
                    copy_s(at + -1)

            run_steps(act, step, -1, B - 1)
            copy_s(At(ITERS - 1, UNROLL - 1))
            for b in range(B - NORM_LAG, B - G):
                normalise(At(ITERS - 1, b % UNROLL))
            for j in range(G - 1):
                if j == G // 2:
                    square_root(LAST, LATE, NG + 1)
                    act.wait_ge(rstd_done, NG + 1)
                    act.wait_ge(shift_done, NG + 1)
                normalise(At(ITERS - 1, UNROLL - G + j))
            act.wait_ge(flag_ready, 1)
            with act.If(act.value_load(flag[0:1, 0:1], min_val=0, max_val=P) > 0):
                with act.Fori(0, B) as b:
                    act.wait_ge(g_dve, b * G_DVE + G_VAR)
                    nc.scalar.activation(g_ln[:, 1:2], g_ln[:, 0:1], ACT.Sqrt).then_inc(g_act, 1)

        def general(dve, b):
            n = [0]

            def link(ins):
                ins.then_inc(g_dve, 1)
                n[0] += 1
                dve.wait_ge(g_dve, b * G_DVE + n[0])

            def v(*a, **k):
                link(nc.vector.tensor_scalar(*a, **k))

            dve.wait_ge(g_loaded, (b + 1) * 32)
            link(nc.vector.tensor_copy(g_a[:, :], gadj[:, :]))
            dve.wait_ge(g_pe, b * 3 + 1)
            link(nc.vector.tensor_copy(g_at[:, :], banks[1][:, 0:N]))
            v(g_tmp[:, :], g_a[:, :], 0.0, float(NUM_REL), ALU.is_lt, ALU.mult)
            link(nc.vector.tensor_tensor(g_tmp[:, :], g_tmp[:, :], g_a[:, :], ALU.add))
            v(g_idx[:, 0, :], g_tmp[:, :], 0.0, float(NUM_REL - 1), ALU.max, ALU.min)
            v(g_tmp[:, :], g_at[:, :], float(NUM_BASE), float(NUM_REL - 1), ALU.add, ALU.min)
            v(g_idx[:, 1, :], g_at[:, :], 0.0, None, ALU.is_gt)
            link(nc.vector.tensor_tensor(g_idx[:, 1, :], g_idx[:, 1, :], g_tmp[:, :], ALU.mult))
            for s, a in enumerate((g_a, g_at)):
                def over_c(t):
                    return t.unsqueeze(1).to_broadcast([P, NUM_REL, N])
                iota = g_iota[:, :].unsqueeze(2).to_broadcast([P, NUM_REL, N])
                link(nc.vector.tensor_tensor(g_hot[:, :, :], over_c(g_idx[:, s, :]), iota, ALU.is_equal))
                link(nc.vector.tensor_tensor(g_hot[:, :, :], g_hot[:, :, :], over_c(a[:, :]), ALU.mult))
                link(nc.vector.tensor_reduce(g_cnt[s][:, 0:NUM_REL], g_hot[:, :, :], AX.X, ALU.add))
                link(nc.vector.tensor_reduce(g_cnt[s][:, NUM_REL:NUM_REL + 1], a[:, :], AX.X, ALU.add))
                d = g_cnt[s][:, NUM_REL:NUM_REL + 1]
                v(g_inv[:, s:s + 1], d, 0.0, None, ALU.is_le)
                link(nc.vector.scalar_tensor_tensor(out=g_inv[:, 2 + s:3 + s], in0=d, scalar=0.0,
                                                    in1=g_inv[:, s:s + 1], op0=ALU.max, op1=ALU.add))
            link(nc.vector.reciprocal(g_inv[:, 0:2], g_inv[:, 2:4]))
            assert n[0] == G_COUNTED
            dve.wait_ge(g_pe, b * 3 + 2)
            for s in range(2):
                link(nc.vector.tensor_copy(g_cnt_t[s][:, :], banks[2 + s][0:NUM_REL + 1, 0:N]))
                link(nc.vector.tensor_copy(g_z[s][:, :], banks[4 + s][:, 0:H]))
            assert n[0] == G_COPIED
            dve.wait_ge(g_pe, b * 3 + 3)
            v(g_t[:, :], banks[6][:, 0:H], g_inv[:, 0:1], None, ALU.mult)
            link(nc.vector.scalar_tensor_tensor(out=g_t[:, :], in0=banks[7][:, 0:H], scalar=g_inv[:, 1:2],
                                                in1=g_t[:, :], op0=ALU.mult, op1=ALU.add))
            link(nc.vector.tensor_tensor(g_t[:, :], banks[0][:, 0:H], g_t[:, :], ALU.add))
            link(nc.vector.bn_stats(g_stats[:, :], g_t[:, :]))
            st, m = g_stats, g_mv
            link(nc.vector.tensor_tensor(m[:, 0:1], st[:, 1:2], st[:, 4:5], ALU.add))
            v(m[:, 0:1], m[:, 0:1], 0.5, None, ALU.mult)
            link(nc.vector.tensor_tensor(m[:, 1:2], st[:, 1:2], st[:, 4:5], ALU.subtract))
            link(nc.vector.tensor_tensor(m[:, 2:3], m[:, 1:2], m[:, 1:2], ALU.mult))
            link(nc.vector.tensor_tensor(m[:, 3:4], st[:, 2:3], st[:, 5:6], ALU.add))
            v(m[:, 4:5], m[:, 3:4], 1.0 / H, EPS, ALU.mult, ALU.add)
            link(nc.vector.scalar_tensor_tensor(out=g_ln[:, 0:1], in0=m[:, 2:3], scalar=0.25, in1=m[:, 4:5],
                                                op0=ALU.mult, op1=ALU.add))
            assert n[0] == G_VAR
            dve.wait_ge(g_act, b + 1)
            link(nc.vector.reciprocal(g_ln[:, 2:3], g_ln[:, 1:2]))
            link(nc.vector.tensor_tensor(g_ln[:, 3:4], g_ln[:, 2:3], g_ln[:, 2:3], ALU.mult))
            link(nc.vector.tensor_tensor(g_ln[:, 4:5], g_ln[:, 3:4], g_ln[:, 0:1], ALU.mult))
            v(g_ln[:, 5:6], g_ln[:, 4:5], -0.5, 1.5, ALU.mult, ALU.add)
            link(nc.vector.tensor_tensor(g_ln[:, 6:7], g_ln[:, 5:6], g_ln[:, 2:3], ALU.mult))
            v(g_y[:, :], g_t[:, :], g_mv[:, 0:1], g_ln[:, 6:7], ALU.subtract, ALU.mult)
            assert n[0] == G_DVE

        @block.vector
        def _(dve):
            nc.vector.memset(odd_sum[:, :], 0.0).then_inc(odd_cleared, 1)
            nc.vector.memset(ones[:, :], 1.0).then_inc(odd_cleared, 1)
            nc.vector.memset(e_sel[:, :, :], 0.0).then_inc(e_sel_zero, 1)
            dve.wait_ge(odd_cleared, 2)
            nc.vector.tensor_copy(ones_r[:, :], ones[:, :]).then_inc(consts_ready, 1)
            dve.wait_ge(table_in, 16)
            for s in range(2):
                nc.vector.tensor_copy(z_hi[s][:, H:H + P], ident).then_inc(consts_ready, 1)

            def low_part_of_x(of):
                wait(dve, x_hi_done, of.graphs())
                wait(dve, *x_parts_free(of))
                nc.vector.tensor_tensor(x_lo[of.slot][:, :], x_in[of.gslot][:, of.j, :], x_hi[of.slot][:, :].bitcast(fp32),
                                        ALU.subtract).then_inc(x_lo_done, 1)

            def low_part_of_z(of):
                wait(dve, z_hi_done, of.graphs())
                nc.vector.tensor_tensor(z_lo[of.slot][:, :], ps_z[of.slot][:, 0:H],
                                        z_hi[of.slot][:, 0:H].bitcast(fp32), ALU.subtract).then_inc(z_lo_done, 1)

            def add_identity():
                for c in range(HC):
                    dve.wait_ge(self_w_in[c], 16)
                    diagonal = w_self[:, c, c * P:(c + 1) * P]
                    nc.vector.tensor_tensor(diagonal, diagonal, ident, ALU.add).then_inc(identity_added, 1)

            def weights(nxt):
                for c in range(HC):
                    dve.wait_ge(self_hi_done, c + 1)
                    nc.vector.tensor_tensor(self_lo[:, c, :], w_self[:, c, :], self_hi[:, c, :].bitcast(fp32),
                                            ALU.subtract).then_inc(self_lo_done, 1)
                for c in range(HC):
                    if c == 1:
                        low_part_of_x(nxt)
                    dve.wait_ge(nb_w_in[c], 32)
                    nc.vector.tensor_tensor(w_nb[:, c, :], w_adj[:, c, :], w_rev[:, c, :],
                                            ALU.add).then_inc(nb_sum_done, 1)
                for c in range(HC):
                    dve.wait_ge(nb_hi_done, c + 1)
                    nc.vector.tensor_tensor(nb_lo[:, c, :], w_nb[:, c, :], nb_hi[:, c, :].bitcast(fp32),
                                            ALU.subtract).then_inc(nb_lo_done, 1)

            def embeddings():
                dve.wait_ge(rel_in, 32)
                dve.wait_ge(e_sel_zero, 1)
                for s, row in enumerate((1, NUM_BASE + 1)):
                    nc.vector.tensor_copy(e_sel[:, s, 0:LOW + 1:LOW],
                                          rel[:, R_E + row:R_E + row + 1].to_broadcast([R, 2])).then_inc(e_sel_ready, 1)

            def bias_side():
                dve.wait_ge(bias_hi_done, 1)
                nc.vector.tensor_copy(bias_rhs[0:LOW, :], bias_all[0:LOW, :].bitcast(fp32)).then_inc(bias_ready, 1)
                nc.vector.tensor_tensor(bias_rhs[LOW:KB, :], ps_c[1][LOW:KB, 0:H], bias_all[LOW:KB, :].bitcast(fp32),
                                        ALU.subtract).then_inc(bias_ready, 1)

            def degree_sums(of):
                s = of.gslot
                wait(dve, adj_loaded[s], of.transfers())
                nc.vector.tensor_reduce(deg[s][:, :], adj_in[s][:, :, :], AX.X, ALU.add).then_inc(deg_done, 1)

            def degree_factors(of):
                s = of.gslot
                wait(dve, deg_row_done, of.group())
                wait(dve, s_done, of.graphs(-1 - G - of.j))
                nc.vector.tensor_scalar(factors[s][:, :, :], ps_deg[0:KB, :].rearrange("p (j n) -> p j n", j=G),
                                        tab[0:KB, C_LIM:C_LIM + 1], tab[0:KB, C_LIM + 1:C_LIM + 2],
                                        ALU.max, ALU.min).then_inc(factors_done, 1)
                wait(dve, deg_done, of.group())
                nc.vector.tensor_scalar(deg[s][:, :], deg[s][:, :], 1.0, None, ALU.max).then_inc(deg_max_done, 1)
                wait(dve, deg_max_done, of.group())
                nc.vector.reciprocal(inv_deg[s][:, :], deg[s][:, :]).then_inc(inv_deg_done, 1)

            def check(of):
                wait(dve, c_done, of.graphs())
                wait(dve, odd_done, of.graphs(-1))
                wait(dve, odd_summed, of.group(-2))
                nc.vector.scalar_tensor_tensor(out=odd_scratch[:, :], in0=ps_c[of.slot][:, H:H + N], scalar=0.0,
                                               in1=a_r[of.gslot][:, of.j, :].bitcast(fp32), op0=ALU.is_gt,
                                               op1=ALU.not_equal,
                                               accum_out=odd[:, of.k % UNROLL:of.k % UNROLL + 1]).then_inc(odd_done, 1)

            def sum_of_checks(of):
                wait(dve, odd_done, of.graphs())
                wait(dve, odd_summed, of.group(-1))
                if of.is_graph(G - 1):
                    wait(dve, odd_cleared, 2)
                nc.vector.tensor_tensor(odd_sum[:, :], odd_sum[:, :], odd[:, of.gslot * G:(of.gslot + 1) * G],
                                        ALU.add).then_inc(odd_summed, 1)

            def graph_sum(of):
                if of.j == 0:
                    wait(dve, inv_deg_done, of.group())
                wait(dve, c_done, of.graphs())
                wait(dve, s_copied, of.graphs())
                wait(dve, y_done, of.graphs(-UNROLL - min(of.k, 0)))
                nc.vector.scalar_tensor_tensor(out=t_sum[of.gslot][:, of.j, :], in0=ps_c[of.slot][:, 0:H],
                                               scalar=inv_deg[of.gslot][:, of.j:of.j + 1],
                                               in1=s_sb[of.slot][:, :], op0=ALU.mult,
                                               op1=ALU.add).then_inc(t_done, 1)

            def statistics(of):
                wait(dve, t_done, of.graphs())
                nc.vector.bn_stats(stats[of.gslot][:, of.j, :], t_sum[of.gslot][:, of.j, :]).then_inc(stats_done, 1)

            def variances(s, part, count):
                m, st, steps = moments[s], stats[s], 5 * count
                nc.vector.tensor_tensor(m[:, 0, part], st[:, part, 1], st[:, part, 4], ALU.add).then_inc(moments_done, 1)
                nc.vector.tensor_tensor(m[:, 1, part], st[:, part, 1], st[:, part, 4],
                                        ALU.subtract).then_inc(moments_done, 1)
                nc.vector.tensor_tensor(m[:, 2, part], st[:, part, 2], st[:, part, 5], ALU.add).then_inc(moments_done, 1)
                wait(dve, moments_done, steps - 3)
                nc.vector.tensor_tensor(m[:, 3, part], m[:, 1, part], m[:, 1, part], ALU.mult).then_inc(moments_done, 1)
                wait(dve, moments_done, steps - 2)
                nc.vector.tensor_scalar(m[:, 4, part], m[:, 2, part], 1.0 / H, EPS,
                                        ALU.mult, ALU.add).then_inc(moments_done, 1)
                wait(dve, moments_done, steps)
                nc.vector.scalar_tensor_tensor(out=var_eps[s][:, part], in0=m[:, 3, part], scalar=0.25,
                                               in1=m[:, 4, part], op0=ALU.mult, op1=ALU.add).then_inc(var_eps_done, 1)

            def inverse_roots(s, part, count):
                w, steps = newton[s], 4 * count
                wait(dve, root_done, count)
                nc.vector.reciprocal(w[:, 0, part], root[s][:, part]).then_inc(newton_done, 1)
                wait(dve, newton_done, steps - 3)
                nc.vector.tensor_tensor(w[:, 1, part], w[:, 0, part], w[:, 0, part], ALU.mult).then_inc(newton_done, 1)
                wait(dve, newton_done, steps - 2)
                nc.vector.tensor_tensor(w[:, 2, part], w[:, 1, part], var_eps[s][:, part],
                                        ALU.mult).then_inc(newton_done, 1)
                wait(dve, newton_done, steps - 1)
                nc.vector.tensor_scalar(w[:, 3, part], w[:, 2, part], -0.5, 1.5, ALU.mult, ALU.add).then_inc(newton_done, 1)
                wait(dve, newton_done, steps)
                nc.vector.tensor_tensor(rstd[s][:, part], w[:, 3, part], w[:, 0, part], ALU.mult).then_inc(rstd_done, 1)
                wait(dve, rstd_done, count)
                nc.vector.scalar_tensor_tensor(out=shift[s][:, part], in0=moments[s][:, 0, part], scalar=-0.5,
                                               in1=rstd[s][:, part], op0=ALU.mult, op1=ALU.mult).then_inc(shift_done, 1)

            def step(at):
                old = at + -1
                if at.is_graph(-1):
                    add_identity()
                if at.j == 0 and at.exists() and not at.is_graph(0):
                    degree_factors(at)
                if (at + 1).exists() and not at.is_graph(0):
                    low_part_of_x(at + 1)
                if at.is_graph(-1):
                    weights(at + 2)
                if at.is_graph(0):
                    embeddings()
                    degree_sums(at)
                if at.is_graph(1):
                    low_part_of_z(at)
                    degree_factors(old)
                    bias_side()
                if at.is_graph(B - 1):
                    dve.wait_ge(stats_done, B - G // 2)
                    variances(LAST, EARLY, NG)
                if old.exists():
                    graph_sum(old)
                    check(old)
                if at.exists() and not at.is_graph(1):
                    low_part_of_z(at)
                if old.exists():
                    statistics(old)
                if at.j == 0 and at.group_exists(-1):
                    sum_of_checks(old)
                    wait(dve, stats_done, old.graphs())
                    variances(1 - at.gslot, slice(0, G), at.group(-1))
                if at.j == 1 and at.group_exists(-1):
                    inverse_roots(1 - at.gslot, slice(0, G), at.group(-1))
                if at.j == 1 and at.group_exists(1) and at.exists():
                    degree_sums(at + (G - 1))
                if at.is_graph(B - 1):
                    inverse_roots(LAST, EARLY, NG)

            run_steps(dve, step, -1, B - 1)

            last = At(ITERS - 1, UNROLL - 1)
            graph_sum(last)
            statistics(last)
            dve.wait_ge(stats_done, B)
            variances(LAST, LATE, NG + 1)
            check(last)
            sum_of_checks(last)
            dve.wait_ge(odd_summed, NG)
            nc.vector.tensor_reduce(odd_total[:, :], odd_sum[:, :], AX.X, ALU.add).then_inc(odd_totalled, 1)
            dve.wait_ge(odd_totalled, 1)
            nc.vector.tensor_scalar(verdict[:, :], odd_total[:, :], 0.0, None, ALU.is_gt).then_inc(verdict_ready, 1)
            inverse_roots(LAST, LATE, NG + 1)
            dve.wait_ge(rstd_done, NG + 1)
            dve.wait_ge(shift_done, NG + 1)
            dve.wait_ge(stored[LAST], 16 * ((NG - 1) // 2))
            nc.vector.tensor_scalar(y_out[LAST][:, G - 1, :], t_sum[LAST][:, G - 1, :], rstd[LAST][:, G - 1:G],
                                    shift[LAST][:, G - 1:G], ALU.mult, ALU.add).then_inc(last_y_done, 1)
            dve.wait_ge(verdict_summed, 1)
            nc.vector.tensor_copy(flag[:, :], ps_deg[0:1, 0:1]).then_inc(flag_ready, 1)

            dve.wait_ge(flag_ready, 1)
            with dve.If(dve.value_load(flag[0:1, 0:1], min_val=0, max_val=P) > 0):
                for s, t in enumerate((ew_r, ew_rr)):
                    dve.wait_ge(g_setup_pe, s + 1)
                    nc.vector.tensor_copy(t[0:NUM_REL, :], banks[2 + s][0:NUM_REL, 0:H]).then_inc(g_setup_dve, 1)
                dve.wait_ge(g_moved, 16 * 6)
                with dve.Fori(0, B) as b:
                    general(dve, b)


def kernel(x, adj, L0_gnn_E, L0_gnn_Wadj, L0_gnn_badj, L0_gnn_Wrev, L0_gnn_brev, L0_gnn_Wself, L0_gnn_bself,
           L0_gnn_Wr, L0_gnn_br, L0_gnn_Wrr, L0_gnn_brr):
    import numpy as np
    import concourse.bacc as bacc
    from concourse.bass_utils import run_bass_kernel_spmd

    x_t = np.asarray(x).reshape(B, N, HC, P).transpose(0, 3, 2, 1).reshape(B, P, HC * N)
    arrays = {"x_t": x_t, "adj": adj}
    for name, a in (("WadjT", L0_gnn_Wadj), ("WrevT", L0_gnn_Wrev), ("WselfT", L0_gnn_Wself)):
        arrays[name] = np.asarray(a).T
    arrays["rel_weights"] = np.concatenate([np.asarray(a).T for a in (L0_gnn_E, L0_gnn_Wr, L0_gnn_Wrr)], axis=1)
    arrays["bias_rows"] = np.stack([np.asarray(a) for a in (L0_gnn_badj, L0_gnn_brev, L0_gnn_bself,
                                                            L0_gnn_br, L0_gnn_brr)])
    arrays["table"], arrays["count_to_80"] = constants()

    nc = bacc.Bacc("TRN2", target_bir_lowering=False, num_devices=1)
    arrays = {name: np.ascontiguousarray(a) for name, a in arrays.items()}
    tensors = {name: nc.dram_tensor(name, a.shape, mybir.dt.from_np(a.dtype), kind="ExternalInput").ap()
               for name, a in arrays.items()}
    out = nc.dram_tensor("out", (B, N, H), fp32, kind="ExternalOutput").ap()
    graph_layer(nc, out=out, **tensors)
    return run_bass_kernel_spmd(nc, [arrays], core_ids=[0]).results[0]["out"]
```
